# Optimizing a Trainium2 kernel written in Bass

```python
import numpy as np
import jax
import jax.numpy as jnp

def _softmax(x, axis=-1):
    return jax.nn.softmax(x, axis=axis)

def _gelu(x):
    return jax.nn.gelu(x, approximate=True)

def _silu(x):
    return jax.nn.silu(x)

def _sigmoid(x):
    return jax.nn.sigmoid(x)

def _layernorm(x, axis=-1, eps=1e-05):
    m = jnp.mean(x, axis=axis, keepdims=True)
    v = jnp.var(x, axis=axis, keepdims=True)
    return (x - m) / jnp.sqrt(v + eps)

def _scatter_add(tgt, idx, src, axis=0):
    return tgt.at[idx].add(src)

def _segment_sum(src, seg, n):
    return jax.ops.segment_sum(src, seg, n)
kernel_name = 'mk_xattn_ffn_d2_seqx_r8_09d9af'

def setup_inputs(seed: int=0):
    np.random.seed(seed)
    _w = jnp.asarray

    def _rec_inputs():
        import jax
        import jax.numpy as jnp
        _rk = jax.random.key(seed)
        x = -0.0002928 + 1 * jax.random.normal(jax.random.fold_in(_rk, 1), (128, 64, 128), jnp.float32)
        _lenS = 64 - jax.random.randint(jax.random.fold_in(_rk, 7), (128,), 0, max(1, 64 // 4) + 1, jnp.int32)
        _lenS2 = 64 - jax.random.randint(jax.random.fold_in(_rk, 8), (128,), 0, max(1, 64 // 4) + 1, jnp.int32)
        _ctx_1024P = jax.random.normal(jax.random.fold_in(_rk, 11), (128, 16, 128), jnp.float32)
        _ctx_1024c = jax.random.dirichlet(jax.random.fold_in(_rk, 511), 0.3 * jnp.ones((16,), jnp.float32), (128, 64))
        _ctx_1024t = jnp.einsum('bsk,bkd->bsd', _ctx_1024c, _ctx_1024P)
        _ctx_1024t = _ctx_1024t * jax.lax.rsqrt(jnp.mean(jnp.square(_ctx_1024t)) + 1e-12) * 0.953939
        ctx_1024 = -1.39393e-06 + 0.999914 * (_ctx_1024t + 0.3 * jax.random.normal(jax.random.fold_in(_rk, 611), (128, 64, 128), jnp.float32))
        return (x, ctx_1024)
    x, ctx_1024 = _rec_inputs()

    def _L0_xattn_setup():
        import jax, jax.numpy as jnp
        import numpy as np
        B, S, H, NH = (2, 256, 128, 4)
        DH = H // NH
        EPS_BACKEND = 1e-06
        EPS_LN = 1e-06

        def _mlstm_parallel_stabilized(q, k, v, igate_preact, fgate_preact):
            b, nh, s, dh = q.shape
            log_fg = jax.nn.log_sigmoid(fgate_preact)
            cs = jnp.concatenate([jnp.zeros((b, nh, 1), q.dtype), jnp.cumsum(log_fg[..., 0], axis=2)], axis=2)
            fg_matrix = cs[:, :, :, None] - cs[:, :, None, :]
            fg_matrix = fg_matrix[:, :, 1:, 1:]
            causal = jnp.tril(jnp.ones((s, s), dtype=bool))
            log_fg_matrix = jnp.where(causal, fg_matrix, -jnp.inf)
            log_D = log_fg_matrix + jnp.swapaxes(igate_preact, -2, -1)
            max_log_D = jnp.max(log_D, axis=-1, keepdims=True)
            D = jnp.exp(log_D - max_log_D)
            qk = jnp.einsum('bhsd,bhtd->bhst', q, k) / jnp.sqrt(jnp.asarray(dh, q.dtype))
            C = qk * D
            normalizer = jnp.maximum(jnp.abs(jnp.sum(C, axis=-1, keepdims=True)), jnp.exp(-max_log_D))
            C_norm = C / (normalizer + EPS_BACKEND)
            return jnp.einsum('bhst,bhtd->bhsd', C_norm, v)

        def _multihead_layernorm(x, scale):
            mean = jnp.mean(x, axis=-1, keepdims=True)
            var = jnp.var(x, axis=-1, keepdims=True)
            xn = (x - mean) * jax.lax.rsqrt(var + EPS_LN)
            return xn * scale.reshape(NH, 1, DH)
        key = jax.random.key(seed)
        kq, kk, kv, kib = jax.random.split(key, 4)
        q = jax.random.normal(kq, (B, S, H), dtype=jnp.float32)
        k = jax.random.normal(kk, (B, S, H), dtype=jnp.float32)
        v = jax.random.normal(kv, (B, S, H), dtype=jnp.float32)
        igate_kernel = jnp.zeros((3 * H, NH), dtype=jnp.float32)
        igate_bias = 0.1 * jax.random.normal(kib, (NH,), dtype=jnp.float32)
        fgate_kernel = jnp.zeros((3 * H, NH), dtype=jnp.float32)
        fgate_bias = jnp.linspace(3.0, 6.0, NH, dtype=jnp.float32)
        outnorm_scale = jnp.ones((H,), dtype=jnp.float32)
        return {'q': q, 'k': k, 'v': v, 'igate_kernel': igate_kernel, 'igate_bias': igate_bias, 'fgate_kernel': fgate_kernel, 'fgate_bias': fgate_bias, 'outnorm_scale': outnorm_scale}
    _L0_xattn_all = _L0_xattn_setup()
    _L0_xattn_in = {k: v for k, v in _L0_xattn_all.items() if k in ('igate_kernel', 'igate_bias', 'fgate_kernel', 'fgate_bias', 'outnorm_scale')}
    del _L0_xattn_all

    def _L0_ffn_setup():
        import jax, jax.numpy as jnp
        import numpy as np
        FP8_MAX = 448.0
        key = jax.random.key(seed)
        k_x, k_w, k_b = jax.random.split(key, 3)
        B, S, IN, OUT = (4, 1024, 128, 128)
        x = jax.random.normal(k_x, (B, S, IN), dtype=jnp.float32)
        w_fp32 = jax.random.normal(k_w, (OUT, IN), dtype=jnp.float32)
        weight_fp8 = w_fp32.astype(jnp.float8_e4m3fn).astype(jnp.float32)
        bias = jax.random.normal(k_b, (OUT,), dtype=jnp.float32)
        input_scale = jnp.ones((1,), dtype=jnp.float32)
        weight_scale = jnp.ones((1,), dtype=jnp.float32)
        return {'x': x, 'weight_fp8': weight_fp8, 'bias': bias, 'input_scale': input_scale, 'weight_scale': weight_scale}
    _L0_ffn_all = _L0_ffn_setup()
    _L0_ffn_in = {k: v for k, v in _L0_ffn_all.items() if k in ('weight_fp8', 'bias', 'input_scale', 'weight_scale')}
    del _L0_ffn_all

    def _L1_xattn_setup():
        import jax, jax.numpy as jnp
        import numpy as np
        P_SIZE = 100
        WINDOW_LENGTH = 2
        STAN_DEV = WINDOW_LENGTH / 2.0
        B, S, T = (4, 512, 256)
        Q_SIZE = C_SIZE = 128
        key = jax.random.key(seed)
        k1, k2, k3, k4, k5 = jax.random.split(key, 5)
        q = jax.random.normal(k1, (B, S, Q_SIZE), dtype=jnp.float32)
        c_t = jax.random.normal(k2, (B, T, C_SIZE), dtype=jnp.float32)
        W_a = jax.random.normal(k3, (C_SIZE, Q_SIZE), dtype=jnp.float32) * 0.02
        W_p = jax.random.normal(k4, (P_SIZE, C_SIZE), dtype=jnp.float32) * 0.02
        V_p = jax.random.normal(k5, (1, P_SIZE), dtype=jnp.float32) * 0.02
        return {'q': q, 'c_t': c_t, 'W_a': W_a, 'W_p': W_p, 'V_p': V_p}
    _L1_xattn_all = _L1_xattn_setup()
    _L1_xattn_in = {k: v for k, v in _L1_xattn_all.items() if k in ('W_a', 'W_p', 'V_p')}
    del _L1_xattn_all

    def _L1_ffn_setup():
        import jax, jax.numpy as jnp
        import numpy as np
        DIM = 128

        def _reference_tuple_inner(x, W_r, W_k, W_v, mu_r, mu_k):
            B, T, C = x.shape
            x_prev = jnp.concatenate([jnp.zeros((B, 1, C), x.dtype), x[:, :-1, :]], axis=1)
            xr = mu_r * x + (1.0 - mu_r) * x_prev
            xk = mu_k * x + (1.0 - mu_k) * x_prev
            r = jax.nn.sigmoid(jnp.einsum('btc,dc->btd', xr, W_r))
            k = jnp.einsum('btc,dc->btd', xk, W_k)
            k_act = jnp.square(jax.nn.relu(k))
            out = r * jnp.einsum('btc,dc->btd', k_act, W_v)
            new_state = x[:, -1, :]
            return (out, new_state)
        key = jax.random.key(seed)
        ks = jax.random.split(key, 6)
        B, T, C = (8, 256, DIM)
        x = jax.random.normal(ks[0], (B, T, C), dtype=jnp.float32)
        s = 1.0 / np.sqrt(C)
        W_r = jax.random.uniform(ks[1], (C, C), jnp.float32, -s, s)
        W_k = jax.random.uniform(ks[2], (C, C), jnp.float32, -s, s)
        W_v = jax.random.uniform(ks[3], (C, C), jnp.float32, -s, s)
        mu_r = jax.random.uniform(ks[4], (C,), jnp.float32)
        mu_k = jax.random.uniform(ks[5], (C,), jnp.float32)
        return {'x': x, 'W_r': W_r, 'W_k': W_k, 'W_v': W_v, 'mu_r': mu_r, 'mu_k': mu_k}
    _L1_ffn_all = _L1_ffn_setup()
    _L1_ffn_in = {k: v for k, v in _L1_ffn_all.items() if k in ('W_r', 'W_k', 'W_v', 'mu_r', 'mu_k')}
    del _L1_ffn_all
    return {'x': x, 'ctx_1024': ctx_1024, 'L0_xattn_igate_kernel': _L0_xattn_in['igate_kernel'], 'L0_xattn_igate_bias': _L0_xattn_in['igate_bias'], 'L0_xattn_fgate_kernel': _L0_xattn_in['fgate_kernel'], 'L0_xattn_fgate_bias': _L0_xattn_in['fgate_bias'], 'L0_xattn_outnorm_scale': _L0_xattn_in['outnorm_scale'], 'L0_ffn_weight_fp8': _L0_ffn_in['weight_fp8'], 'L0_ffn_bias': _L0_ffn_in['bias'], 'L0_ffn_input_scale': _L0_ffn_in['input_scale'], 'L0_ffn_weight_scale': _L0_ffn_in['weight_scale'], 'L1_xattn_W_a': _L1_xattn_in['W_a'], 'L1_xattn_W_p': _L1_xattn_in['W_p'], 'L1_xattn_V_p': _L1_xattn_in['V_p'], 'L1_ffn_W_r': _L1_ffn_in['W_r'], 'L1_ffn_W_k': _L1_ffn_in['W_k'], 'L1_ffn_W_v': _L1_ffn_in['W_v'], 'L1_ffn_mu_r': _L1_ffn_in['mu_r'], 'L1_ffn_mu_k': _L1_ffn_in['mu_k']}

def reference(x, ctx_1024, L0_xattn_igate_kernel, L0_xattn_igate_bias, L0_xattn_fgate_kernel, L0_xattn_fgate_bias, L0_xattn_outnorm_scale, L0_ffn_weight_fp8, L0_ffn_bias, L0_ffn_input_scale, L0_ffn_weight_scale, L1_xattn_W_a, L1_xattn_W_p, L1_xattn_V_p, L1_ffn_W_r, L1_ffn_W_k, L1_ffn_W_v, L1_ffn_mu_r, L1_ffn_mu_k):
    import jax
    import jax.numpy as jnp

    def _L0_xattn_ref(q, k, v, igate_kernel, igate_bias, fgate_kernel, fgate_bias, outnorm_scale):
        import jax, jax.numpy as jnp
        import numpy as np
        B, S, H, NH = (2, 256, 128, 4)
        DH = H // NH
        EPS_BACKEND = 1e-06
        EPS_LN = 1e-06

        def _mlstm_parallel_stabilized(q, k, v, igate_preact, fgate_preact):
            b, nh, s, dh = q.shape
            log_fg = jax.nn.log_sigmoid(fgate_preact)
            cs = jnp.concatenate([jnp.zeros((b, nh, 1), q.dtype), jnp.cumsum(log_fg[..., 0], axis=2)], axis=2)
            fg_matrix = cs[:, :, :, None] - cs[:, :, None, :]
            fg_matrix = fg_matrix[:, :, 1:, 1:]
            causal = jnp.tril(jnp.ones((s, s), dtype=bool))
            log_fg_matrix = jnp.where(causal, fg_matrix, -jnp.inf)
            log_D = log_fg_matrix + jnp.swapaxes(igate_preact, -2, -1)
            max_log_D = jnp.max(log_D, axis=-1, keepdims=True)
            D = jnp.exp(log_D - max_log_D)
            qk = jnp.einsum('bhsd,bhtd->bhst', q, k) / jnp.sqrt(jnp.asarray(dh, q.dtype))
            C = qk * D
            normalizer = jnp.maximum(jnp.abs(jnp.sum(C, axis=-1, keepdims=True)), jnp.exp(-max_log_D))
            C_norm = C / (normalizer + EPS_BACKEND)
            return jnp.einsum('bhst,bhtd->bhsd', C_norm, v)

        def _multihead_layernorm(x, scale):
            mean = jnp.mean(x, axis=-1, keepdims=True)
            var = jnp.var(x, axis=-1, keepdims=True)
            xn = (x - mean) * jax.lax.rsqrt(var + EPS_LN)
            return xn * scale.reshape(NH, 1, DH)
        b, s, h = q.shape
        gate_in = jnp.concatenate([q, k, v], axis=-1)
        ig = gate_in @ igate_kernel + igate_bias
        fg = gate_in @ fgate_kernel + fgate_bias
        ig = jnp.transpose(ig, (0, 2, 1))[..., None]
        fg = jnp.transpose(fg, (0, 2, 1))[..., None]
        qh = jnp.transpose(q.reshape(b, s, NH, DH), (0, 2, 1, 3))
        kh = jnp.transpose(k.reshape(b, s, NH, DH), (0, 2, 1, 3))
        vh = jnp.transpose(v.reshape(b, s, NH, DH), (0, 2, 1, 3))
        hs = _mlstm_parallel_stabilized(qh, kh, vh, ig, fg)
        hn = _multihead_layernorm(hs, outnorm_scale)
        return jnp.transpose(hn, (0, 2, 1, 3)).reshape(b, s, h)

    def _L0_ffn_ref(x, weight_fp8, bias, input_scale, weight_scale):
        import jax, jax.numpy as jnp
        import numpy as np
        FP8_MAX = 448.0
        x_q = jnp.clip(x / input_scale, -FP8_MAX, FP8_MAX)
        x_dq = x_q.astype(jnp.float8_e4m3fn).astype(x.dtype) * input_scale
        w_dq = weight_fp8 * weight_scale
        out = jnp.einsum('bsi,oi->bso', x_dq, w_dq) + bias
        return out

    def _L1_xattn_ref(q, c_t, W_a, W_p, V_p):
        import jax, jax.numpy as jnp
        import numpy as np
        P_SIZE = 100
        WINDOW_LENGTH = 2
        STAN_DEV = WINDOW_LENGTH / 2.0
        B, S, T = (4, 512, 256)
        Q_SIZE = C_SIZE = 128
        Bq, Sq, _ = q.shape
        hid = jnp.tanh(jnp.einsum('btc,pc->btp', c_t, W_p))
        p_t = Sq * jax.nn.sigmoid(jnp.einsum('btp,op->bto', hid, V_p))
        win_low = p_t.astype(jnp.int32) - WINDOW_LENGTH
        window = win_low + jnp.arange(2 * WINDOW_LENGTH, dtype=jnp.int32)
        window = jnp.clip(window, 0, Sq - 1)
        qw = jnp.take_along_axis(q[:, None, :, :], window[:, :, :, None], axis=2)
        scores = jnp.einsum('btwq,cq,btc->btw', qw, W_a, c_t)
        s_pos = window.astype(jnp.float32)
        gauss = jnp.exp(-jnp.square(s_pos - p_t) / (2.0 * STAN_DEV ** 2))
        a_t = jax.nn.softmax(scores, axis=-1) * gauss
        s_t = jnp.einsum('btw,btwq->btq', a_t, qw)
        return s_t

    def _L1_ffn_ref(x, W_r, W_k, W_v, mu_r, mu_k):
        import jax, jax.numpy as jnp
        import numpy as np
        DIM = 128

        def _reference_tuple_inner(x, W_r, W_k, W_v, mu_r, mu_k):
            B, T, C = x.shape
            x_prev = jnp.concatenate([jnp.zeros((B, 1, C), x.dtype), x[:, :-1, :]], axis=1)
            xr = mu_r * x + (1.0 - mu_r) * x_prev
            xk = mu_k * x + (1.0 - mu_k) * x_prev
            r = jax.nn.sigmoid(jnp.einsum('btc,dc->btd', xr, W_r))
            k = jnp.einsum('btc,dc->btd', xk, W_k)
            k_act = jnp.square(jax.nn.relu(k))
            out = r * jnp.einsum('btc,dc->btd', k_act, W_v)
            new_state = x[:, -1, :]
            return (out, new_state)
        return _reference_tuple_inner(x, W_r, W_k, W_v, mu_r, mu_k)[0]
    x = x + _L0_xattn_ref(_layernorm(x, axis=-1), ctx_1024, ctx_1024, L0_xattn_igate_kernel, L0_xattn_igate_bias, L0_xattn_fgate_kernel, L0_xattn_fgate_bias, L0_xattn_outnorm_scale)
    x = x + _L0_ffn_ref(_layernorm(x, axis=-1), L0_ffn_weight_fp8, L0_ffn_bias, L0_ffn_input_scale, L0_ffn_weight_scale)
    x = x + _L1_xattn_ref(ctx_1024, _layernorm(x, axis=-1), L1_xattn_W_a, L1_xattn_W_p, L1_xattn_V_p)
    x = x + _L1_ffn_ref(_layernorm(x, axis=-1), L1_ffn_W_r, L1_ffn_W_k, L1_ffn_W_v, L1_ffn_mu_r, L1_ffn_mu_k)
    return x

_drawn_inputs = setup_inputs


def setup_inputs(seed=0):
    import zlib

    import numpy as np

    out = dict(_drawn_inputs(seed))
    spreads = {'L0_xattn_igate_kernel': (0.0, 0.1),
     'L0_xattn_fgate_kernel': (0.0, 0.1),
     'L0_xattn_outnorm_scale': (1.0, 0.2)}
    factors = {'L0_xattn_igate_bias': 64.0,
     'L1_xattn_W_p': 2.764,
     'L1_ffn_W_r': 8.0,
     'L1_ffn_W_k': 8.0,
     'L1_ffn_W_v': 7.918,
     'L1_ffn_mu_r': 8.0,
     'L1_ffn_mu_k': 8.0}
    for name, (base, spread) in spreads.items():
        noise = np.random.default_rng([zlib.crc32(name.encode()), seed]).standard_normal(out[name].shape)
        drawn = base * np.exp(spread * noise) if base else spread * noise
        out[name] = jnp.asarray(drawn.astype(out[name].dtype))
    for name, factor in factors.items():
        out[name] = (out[name] * factor).astype(out[name].dtype)
    return out
```

```python
from contextlib import ExitStack

import concourse.bass as bass
from concourse import mybir

ALU = mybir.AluOpType
ACT = mybir.ActivationFunctionType
F32 = mybir.dt.float32
BF16 = mybir.dt.bfloat16
U32 = mybir.dt.uint32
AX_X = mybir.AxisListType.X

P = 128
S = 64
D = 128
NH = 4
DH = D // NH
TPG = 4
GC = TPG * D
HID = 100
BIG = 1.0e30
EPS_NORM = 1e-5
EPS_HEAD = 1e-6
EPS_BACKEND = 1e-6
FP8_MAX = 448.0
ROUND_INT = 8388608.0
ROUND_E4M3 = 1.5 * 2.0**20
E4M3_MIN_NORMAL = 2.0**-6
ATANH = (1.0, 0.33333158, 0.20012427, 0.13980709, 0.14087329)
MIN_LOG = -34.0


def xattn_ffn_two_layers(
    nc, x, ctx, igate_kernel, igate_bias, fgate_kernel, fgate_bias, outnorm_scale,
    weight_fp8, ffn_bias, input_scale, weight_scale, W_a, W_p, V_p, W_r, W_k, W_v, mu_r, mu_k, out,
):
    B = x.shape[0]
    NT = B * S // P
    NG = NT // TPG
    LAST = 3
    STEADY = LAST + 1

    x_dram = x.rearrange("b s d -> (b s) d").rearrange("(g j p) d -> g p j d", j=TPG, p=P)
    ctx_dram = ctx.rearrange("b s d -> (b s) d").rearrange("(g j p) d -> g p j d", j=TPG, p=P)
    out_dram = out.rearrange("b s d -> (b s) d").rearrange("(g j p) d -> g p j d", j=TPG, p=P)

    with ExitStack() as stack:
        def sb(name, shape, dt=F32):
            return stack.enter_context(nc.sbuf_tensor(name, shape, dt))

        def sem(name):
            return stack.enter_context(nc.semaphore(name))

        banks = stack.enter_context(nc.psum_tensor("banks", [P, 8, 512], F32))
        bank = [banks[:, i, :] for i in range(8)]

        x_all = sb("x_all", [P, NG, TPG, D])
        kw_all = sb("kw_all", [P, NG, TPG * P])

        ident = sb("ident", [P, P])
        ident_bf = sb("ident_bf", [P, P], BF16)
        ones_bf = sb("ones_bf", [P, P], BF16)
        cum = sb("cum", [P, S])
        neg_cum = sb("neg_cum", [P, S])
        pick = sb("pick", [P, S])
        causal = sb("causal", [P, NH // 2, TPG, S], BF16)
        batch_mask = sb("batch_mask", [P, 4, 2])
        row_mask = sb("row_mask", [P, 2])
        pick_row = sb("pick_row", [P, 16, 2, S], BF16)
        row_cols = sb("row_cols", [P, 2, 2, TPG, S], BF16)
        back = sb("back", [32, 2, 16])
        iota = sb("iota", [P, S])
        eps_col = sb("eps_col", [P, 1])
        spare_pool = sb("spare_pool", [P, 1])
        spare = sb("spare", [P, 1])
        half_power = sb("half_power", [P, 16])

        NW = 6
        WA, WP, WR, WK, WV, WF = range(NW)
        w_raw = sb("w_raw", [P, NW, D])
        w_t = sb("w_t", [P, NW, D])
        vp_col = sb("vp_col", [HID, 1])
        igk = sb("igk", [P, 3, NH])
        fgk = sb("fgk", [P, 3, NH])
        gate_w_q = sb("gate_w_q", [P, 12])
        gate_w_c = sb("gate_w_c", [P, 12])
        gate_bias = sb("gate_bias", [P, 2 * NH])
        head_scale = sb("head_scale", [P, D])
        in_scale = sb("in_scale", [P, 1])
        w_scale = sb("w_scale", [P, 1])
        in_scale_inv = sb("in_scale_inv", [P, 1])
        mu = sb("mu", [P, 2])
        w_rest = sb("w_rest", [P, 2, D])
        w_parts = sb("w_parts", [P, 3, D], BF16)
        bias_rows = sb("bias_rows", [P, D])
        bias_tmp = sb("bias_tmp", [P, 2, D], BF16)
        bias_parts = sb("bias_parts", [P, TPG, D], BF16)

        stats = [sb(f"stats_{s}", [P, TPG, 6]) for s in "abcd"]
        mv = [sb(f"mv_{s}", [P, TPG, 2]) for s in "abcd"]
        var_eps = [sb(f"var_eps_{s}", [P, TPG]) for s in "abcd"]
        rstd = [sb(f"rstd_{s}", [P, TPG]) for s in "abcd"]
        normed = [sb(f"normed_{s}", [P, TPG, D]) for s in "abcd"]

        ctx_a = sb("ctx_a", [P, TPG, D])
        q_t = sb("q_t", [P, TPG * P])
        ctx_t = sb("ctx_t", [P, TPG * P])
        gates = sb("gates", [P, 2, TPG, NH])
        v_mean = sb("v_mean", [P, 16])
        neg_abs = sb("neg_abs", [P, 16])
        low = sb("low", [P, 16])
        gate_u = sb("gate_u", [P, 16])
        gate_den = sb("gate_den", [P, 16])
        gate_rec = sb("gate_rec", [P, 16])
        gate_z = sb("gate_z", [P, 16])
        gate_z2 = sb("gate_z2", [P, 16])
        gate_q = [sb(f"gate_q{k}", [P, 16]) for k in range(6)]
        gates_exp = sb("gates_exp", [P, 2, 8, 16])
        a_row = sb("a_row", [P, S])
        run_max = sb("run_max", [P, S])
        max_log = sb("max_log", [P, S])
        exp_row = sb("exp_row", [P, S])
        rest = sb("rest", [P, 3, S])
        part_tmp = sb("part_tmp", [P, 2, 3, S], BF16)
        parts = sb("parts", [P, 3, S], BF16)
        v_aug = sb("v_aug", [P, TPG, NH, DH + 1])
        decay = sb("decay", [P, 2, 2, TPG, S])
        weights = sb("weights", [P, 2, 2, TPG, S])
        h_sq = sb("h_sq", [P, 16, DH])
        h_ss = sb("h_ss", [P, 16])
        floor_n = sb("floor_n", [P, 16])
        norm_n = sb("norm_n", [P, 16])
        norm_e = sb("norm_e", [P, 16])
        norm_q = sb("norm_q", [P, 16])
        h_var = sb("h_var", [P, 16])
        h_rstd = sb("h_rstd", [P, 16])
        h_n = sb("h_n", [P, 16, DH])
        h_s = sb("h_s", [P, TPG, D])

        scale_b = sb("scale_b", [P, TPG])
        clipped = sb("clipped", [P, GC])
        expo = sb("expo", [P, GC])
        magic = sb("magic", [P, GC])
        shifted = sb("shifted", [P, GC])
        x_q = sb("x_q", [P, TPG, D], BF16)
        x_q_t = sb("x_q_t", [P, TPG * P], BF16)

        ctx_c = sb("ctx_c", [P, TPG, D])
        kw_c = sb("kw_c", [P, TPG * P])
        c_t = sb("c_t", [P, TPG * P])
        hid = sb("hid", [HID, TPG * P])
        tanh_z = sb("tanh_z", [P, TPG])
        pos = sb("pos", [P, TPG])
        pos_r = sb("pos_r", [P, TPG])
        pos_gt = sb("pos_gt", [P, TPG])
        pos_fl = sb("pos_fl", [P, TPG])
        edge = sb("edge", [P, TPG, 2])
        off = sb("off", [P, TPG, S])
        off_sq = sb("off_sq", [P, TPG, S])
        outside = sb("outside", [P, TPG, S])
        dist = sb("dist", [P, TPG, S])
        dist2 = sb("dist2", [P, TPG, S])
        gauss = sb("gauss", [P, TPG, S])
        scm = sb("scm", [P, TPG, S])
        sc_max = sb("sc_max", [P, TPG])
        scs = sb("scs", [P, TPG, S])
        prob = sb("prob", [P, TPG, S])
        den = sb("den", [P, TPG])
        rden = sb("rden", [P, TPG])
        pg = sb("pg", [P, TPG, S])
        att = sb("att", [P, TPG, S])
        att_t = sb("att_t", [P, TPG, S])

        NB = 2 * TPG
        x_pad = sb("x_pad", [P, NB, S + 1])
        diff = sb("diff", [P, NB, S])
        x_r = sb("x_r", [P, NB, S])
        x_k = sb("x_k", [P, NB, S])
        k_relu = sb("k_relu", [P, GC])
        k_act = sb("k_act", [P, GC])
        r_tanh = sb("r_tanh", [P, GC])
        y = sb("y", [P, GC])

        x_loaded, ctx_a_loaded, ctx_c_loaded = sem("x_loaded"), sem("ctx_a_loaded"), sem("ctx_c_loaded")
        w_loaded, small_loaded, bias_loaded = sem("w_loaded"), sem("small_loaded"), sem("bias_loaded")
        ident_ready, consts_step, consts_ready = sem("ident_ready"), sem("consts_step"), sem("consts_ready")
        w_transposed, w_evac, split_step, weights_ready, bias_cleared = (
            sem("w_transposed"), sem("w_evac"), sem("split_step"), sem("weights_ready"), sem("bias_cleared"))
        stats_done = [sem(f"stats_{s}_done") for s in "abcd"]
        mean_ready = [sem(f"mean_{s}_ready") for s in "abcd"]
        eps_added = [sem(f"eps_{s}_added") for s in "abcd"]
        rstd_ready = [sem(f"rstd_{s}_ready") for s in "abcd"]
        normed_ready = [sem(f"normed_{s}_ready") for s in "abcd"]
        names = """
            q_in_psum ctx_in_psum q_t_ready ctx_t_ready gates_in_psum kw_in_psum kw_ready
            gates_ready v_mean_ready neg_abs_ready low_ready gate_u_ready gate_den_ready gate_rec_ready
            gate_z_ready gate_z2_ready gate_q0 gate_q1 gate_q2 gate_q3 gate_q4 log_f_ready
            gates_exp_ready rows_in_psum a_row_ready rest_ready run_max_ready sum_row_ready max_log_ready
            exp_row_ready part0_ready rest1_ready part1_ready rest2_ready parts_ready v_aug_ready
            head_scores_done decay_log_in_psum decay_ready weights_ready_a heads_in_psum
            h_sq_ready h_ss_ready floor_n_ready norm_n_ready norm_e_ready norm_q_ready h_var_ready h_rstd_ready
            h_n_ready h_s_ready stage_a_done
            scale_b_ready clipped_ready expo_ready magic_ready shifted_ready x_q_ready
            x_q_in_psum x_q_t_ready ffn_in_psum stage_b_done
            c_in_psum c_t_ready hid_in_psum hid_ready z_in_psum tanh_z_ready pos_ready pos_r_ready pos_gt_ready
            pos_fl_ready edge_ready off_ready off_sq_ready outside_ready dist_ready dist2_ready gauss_ready
            kw_c_ready win_scores_in_psum scm_ready sc_max_ready scs_ready prob_ready edges_ready den_ready
            rden_ready pg_ready att_ready att_in_psum att_t_ready win_in_psum stage_c_done
            x4_in_psum x4_ready diff_ready x_r_ready x_k_ready k_in_psum k_relu_ready k_act_ready
            r_in_psum r_tanh_ready v_in_psum y_ready stage_d_done stored
        """.split()
        s = {n: sem(n) for n in names}

        (q_in_psum, ctx_in_psum, q_t_ready, ctx_t_ready, gates_in_psum, kw_in_psum, kw_ready,
         gates_ready, v_mean_ready, neg_abs_ready, low_ready, gate_u_ready, gate_den_ready, gate_rec_ready,
         gate_z_ready, gate_z2_ready, gate_q0, gate_q1, gate_q2, gate_q3, gate_q4, log_f_ready,
         gates_exp_ready, rows_in_psum, a_row_ready, rest_ready, run_max_ready, sum_row_ready, max_log_ready,
         exp_row_ready, part0_ready, rest1_ready, part1_ready, rest2_ready, parts_ready, v_aug_ready,
         head_scores_done, decay_log_in_psum, decay_ready, weights_ready_a, heads_in_psum,
         h_sq_ready, h_ss_ready, floor_n_ready, norm_n_ready, norm_e_ready, norm_q_ready, h_var_ready, h_rstd_ready,
         h_n_ready, h_s_ready, stage_a_done,
         scale_b_ready, clipped_ready, expo_ready, magic_ready, shifted_ready, x_q_ready,
         x_q_in_psum, x_q_t_ready, ffn_in_psum, stage_b_done,
         c_in_psum, c_t_ready, hid_in_psum, hid_ready, z_in_psum, tanh_z_ready, pos_ready, pos_r_ready, pos_gt_ready,
         pos_fl_ready, edge_ready, off_ready, off_sq_ready, outside_ready, dist_ready, dist2_ready, gauss_ready,
         kw_c_ready, win_scores_in_psum, scm_ready, sc_max_ready, scs_ready, prob_ready, edges_ready, den_ready,
         rden_ready, pg_ready, att_ready, att_in_psum, att_t_ready, win_in_psum, stage_c_done,
         x4_in_psum, x4_ready, diff_ready, x_r_ready, x_k_ready, k_in_psum, k_relu_ready, k_act_ready,
         r_in_psum, r_tanh_ready, v_in_psum, y_ready, stage_d_done, stored) = [s[n] for n in names]
        A_, B_, C_, D_ = range(4)

        bank_q = bank[0]
        bank_ctx = bank[1]
        gates_ps = bank[2][:, 0:48].rearrange("p (j c) -> p j c", j=TPG)
        rows_ps = bank[3][:, 0:2 * S].rearrange("p (k s) -> p k s", k=2)
        score_ps = [bank[k][:, :].rearrange("p (u j s) -> p u j s", u=2, j=TPG) for k in (0, 1)]
        decay_ps = [bank[k][:, :].rearrange("p (u j s) -> p u j s", u=2, j=TPG) for k in (2, 3)]
        heads_ps = banks[:, 2:4, 0:8 * (DH + 1)].rearrange("p k (c d) -> p k c d", d=DH + 1)
        exp_col_ps = bank[3][:, 480:496]
        ffn_ps = bank[4]
        xq_ps = bank[4][:, :].bitcast(BF16)[:, 0:GC]
        win_ps = bank[5][:, 0:TPG * S].rearrange("p (j s) -> p j s", j=TPG)
        z_ps = bank[5][:, TPG * S:TPG * S + TPG]
        att_ps = bank[6][:, 0:TPG * S].rearrange("p (j s) -> p j s", j=TPG)

        NSMALL = 10

        def started(g):
            return not (isinstance(g, int) and g <= 0)

        def steps(engine, step):
            for i in range(STEADY):
                step(i)
            with engine.Fori(STEADY, NG) as i:
                step(i)
            for i in range(NG, NG + LAST):
                step(i)

        def works(i, skew):
            return not isinstance(i, int) or 0 <= i - skew < NG

        block = stack.enter_context(nc.Block())

        @block.sync
        def _(sp):
            sp.dma_start(x_all[:, 0, :, :], x_dram[0]).then_inc(x_loaded, 16)
            sp.dma_start(ctx_a[:, :, :], ctx_dram[0]).then_inc(ctx_a_loaded, 16)
            for n, w in ((WF, weight_fp8), (WA, W_a), (WP, W_p), (WR, W_r), (WK, W_k), (WV, W_v)):
                rows = w.shape[0]
                sp.dma_start(w_raw[0:rows, n, :], w).then_inc(w_loaded, 16)
            sp.dma_start(igk[:, :, :], igate_kernel.rearrange("(k c) h -> c k h", c=D)).then_inc(small_loaded, 16)
            sp.dma_start(fgk[:, :, :], fgate_kernel.rearrange("(k c) h -> c k h", c=D)).then_inc(small_loaded, 16)
            sp.dma_start(gate_bias[:, 0:NH], igate_bias.partition_broadcast(P)).then_inc(small_loaded, 16)
            sp.dma_start(gate_bias[:, NH:2 * NH], fgate_bias.partition_broadcast(P)).then_inc(small_loaded, 16)
            sp.dma_start(head_scale[:, :], outnorm_scale.partition_broadcast(P)).then_inc(small_loaded, 16)
            sp.dma_start(in_scale[:, :], input_scale.partition_broadcast(P)).then_inc(small_loaded, 16)
            sp.dma_start(w_scale[:, :], weight_scale.partition_broadcast(P)).then_inc(small_loaded, 16)
            sp.dma_start(mu[:, 0:1], mu_r.rearrange("(c a) -> c a", a=1)).then_inc(small_loaded, 16)
            sp.dma_start(mu[:, 1:2], mu_k.rearrange("(c a) -> c a", a=1)).then_inc(small_loaded, 16)
            sp.dma_start(vp_col[:, :], V_p.rearrange("a p -> p a")).then_inc(small_loaded, 16)
            sp.wait_ge(bias_cleared, 1)
            for p in (0, 64, 96):
                sp.dma_start(bias_rows[p:p + 1, :], ffn_bias.rearrange("(a d) -> a d", a=1)).then_inc(bias_loaded, 16)

            def step(i):
                if works(i + 1, 0) and not (not isinstance(i, int) and False):
                    if isinstance(i, int) and i + 1 >= NG:
                        return_load = False
                    else:
                        return_load = True
                else:
                    return_load = False
                if return_load:
                    sp.wait_ge(x_loaded, 16 * (i + 1))
                    sp.dma_start(x_all[:, next_group(i), :, :], x_dram[next_group(i)]).then_inc(x_loaded, 16)
                    sp.wait_ge(ctx_in_psum, i + 1)
                    sp.wait_ge(v_aug_ready, i + 1)
                    sp.dma_start(ctx_a[:, :, :], ctx_dram[next_group(i)]).then_inc(ctx_a_loaded, 16)
                if works(i, 1):
                    g = i - 1
                    if started(g):
                        sp.wait_ge(win_in_psum, g)
                    sp.dma_start(ctx_c[:, :, :], ctx_dram[g]).then_inc(ctx_c_loaded, 16)
                if works(i, LAST):
                    g = i - LAST
                    sp.wait_ge(stage_d_done, g + 1)
                    sp.dma_start(out_dram[g], x_all[:, g, :, :]).then_inc(stored, 16)

            def next_group(i):
                return i + 1

            for i in range(STEADY):
                step(i)
            with sp.Fori(STEADY, NG - 1) as i:
                step(i)
            for i in range(NG - 1, NG + LAST):
                step(i)
            sp.wait_ge(stored, 16 * NG)

        @block.gpsimd
        def _(pool):
            pool.memset(bias_rows[:, :], 0.0).then_inc(bias_cleared, 1)
            pool.wait_ge(bias_cleared, 1)
            made = [0]

            def then(instruction):
                made[0] += 1
                instruction.then_inc(consts_step, 1)
                pool.wait_ge(consts_step, made[0])

            def cut(view, pattern, op, fill, base, cm=1):
                then(pool.affine_select(out=view, in_=view, pattern=pattern, compare_op=op, fill=fill,
                                        base=base, channel_multiplier=cm))

            then(pool.memset(ident[:, :], 1.0))
            cut(ident[:, :], [[-1, P]], ALU.is_equal, 0.0, 0)
            pool.tensor_copy(ident_bf[:, :], ident[:, :]).then_inc(ident_ready, 1)
            pool.wait_ge(ident_ready, 1)
            for c in (ones_bf, cum, pick):
                then(pool.memset(c[:, :], 1.0))
            then(pool.memset(neg_cum[:, :], -1.0))
            then(pool.memset(half_power[:, :], -0.5))
            then(pool.memset(eps_col[:, :], EPS_NORM))
            then(pool.memset(causal[:, :, :, :], 0.0))
            then(pool.memset(batch_mask[:, :, :], 0.0))
            then(pool.memset(row_mask[:, :], 1.0))
            then(pool.memset(pick_row[:, :, :, :], 0.0))
            then(pool.memset(row_cols[:, :, :, :, :], 0.0))
            then(pool.memset(back[:, :, :], 0.0))
            then(pool.memset(x_pad[:, :, 0:1], 0.0))
            then(pool.memset(v_aug[:, :, :, DH:DH + 1], 1.0))
            then(pool.iota(iota[:, :], [[1, S]], base=0, channel_multiplier=0, allow_small_or_imprecise_dtypes=True))
            for b in range(2):
                rows = slice(S * b, S * b + S)
                cut(cum[rows, :], [[1, S]], ALU.is_ge, 0.0, 0, -1)
                cut(neg_cum[rows, :], [[1, S]], ALU.is_ge, 0.0, 0, -1)
                cut(pick[rows, :], [[1, S]], ALU.is_equal, 0.0, 0, -1)
                cut(causal[rows, :, :, :].rearrange("p u j s -> p (u j) s"), [[0, 2 * TPG], [1, S]],
                    ALU.is_ge, -BIG, 0, -1)
                then(pool.memset(batch_mask[rows, :, b:b + 1], 1.0))
                cut(back[:, b, :], [[-1, 16]], ALU.not_equal, 1.0, -16 * b)
            for quad in range(4):
                rows = slice(32 * quad, 32 * quad + 32)
                cut(row_mask[rows, :], [[-16, 2]], ALU.is_ge, 0.0, 0)
                cut(row_mask[rows, :], [[16, 2]], ALU.is_ge, 0.0, 15, -1)
                if quad == 1:
                    continue
                cut(pick_row[rows, :, :, :], [[-1, 16], [-16, 2], [0, S]], ALU.not_equal, 1.0, 0)
                for k in range(2):
                    for u in range(2):
                        for b in range(2):
                            cut(row_cols[rows, k, u, :, :], [[-4, TPG], [0, S]], ALU.not_equal, 1.0,
                                -(2 * u + k) - 16 * b)
            pool.memset(spare_pool[:, :], 0.0).then_inc(consts_ready, 1)

            def norm_scale(st, g):
                if started(g):
                    pool.wait_ge(rstd_ready[st], g)
                pool.wait_ge(mean_ready[st], 4 * g + 4)
                pool.tensor_tensor(var_eps[st][:, :], mv[st][:, :, 1], eps_col[:, 0:1].to_broadcast([P, TPG]),
                                   ALU.add).then_inc(eps_added[st], 1)
                pool.wait_ge(eps_added[st], g + 1)
                if started(g):
                    pool.wait_ge(normed_ready[st], 4 * g)
                pool.tensor_tensor(rstd[st][:, :], var_eps[st][:, :], half_power[:, 0:TPG], ALU.pow)\
                    .then_inc(rstd_ready[st], 1)

            def step(i):
                a, b, c, d = i, i - 1, i - 2, i - 3
                if works(i, 3):
                    norm_scale(D_, d)
                if works(i, 2):
                    norm_scale(C_, c)
                if works(i, 1):
                    norm_scale(B_, b)
                    pool.wait_ge(rstd_ready[B_], b + 1)
                    if started(b):
                        pool.wait_ge(normed_ready[B_], 4 * b)
                    pool.tensor_tensor(scale_b[:, :], rstd[B_][:, :], in_scale_inv[:, 0:1].to_broadcast([P, TPG]),
                                       ALU.mult).then_inc(scale_b_ready, 1)
                if works(i, 0):
                    norm_scale(A_, a)
                if works(i, 3):
                    pool.wait_ge(x4_ready, d + 1)
                    if started(d):
                        pool.wait_ge(x_k_ready, d)
                    pool.tensor_tensor(diff[:, :, :], x_pad[:, :, 1:S + 1], x_pad[:, :, 0:S], ALU.subtract)\
                        .then_inc(diff_ready, 1)
                if works(i, 2):
                    if started(c):
                        pool.wait_ge(win_scores_in_psum, c)
                    pool.wait_ge(kw_ready, c + 1)
                    pool.tensor_copy(kw_c[:, :], kw_all[:, c, :]).then_inc(kw_c_ready, 1)
                if works(i, 0):
                    pool.wait_ge(v_mean_ready, a + 1)
                    pool.wait_ge(ctx_a_loaded, 16 * (a + 1))
                    if started(a):
                        pool.wait_ge(heads_in_psum, a)
                    pool.tensor_tensor(v_aug[:, :, :, :].rearrange("p j h d -> p (j h) d")[:, :, 0:DH],
                                       ctx_a[:, :, :].rearrange("p j (h d) -> p (j h) d", h=NH),
                                       v_mean[:, :].unsqueeze(2).to_broadcast([P, 16, DH]),
                                       ALU.subtract).then_inc(v_aug_ready, 1)
                if works(i, 3):
                    pool.wait_ge(k_relu_ready, d + 1)
                    if started(d):
                        pool.wait_ge(v_in_psum, d)
                    pool.tensor_tensor(k_act[:, :], k_relu[:, :], k_relu[:, :], ALU.mult).then_inc(k_act_ready, 1)
                if works(i, 2):
                    pool.wait_ge(pos_ready, c + 1)
                    if started(c):
                        pool.wait_ge(dist2_ready, c)
                    pool.tensor_tensor(dist[:, :, :], iota[:, :].unsqueeze(1).to_broadcast([P, TPG, S]),
                                       pos[:, :].unsqueeze(2).to_broadcast([P, TPG, S]),
                                       ALU.subtract).then_inc(dist_ready, 1)
                    pool.wait_ge(dist_ready, c + 1)
                    if started(c):
                        pool.wait_ge(gauss_ready, c)
                    pool.tensor_tensor(dist2[:, :, :], dist[:, :, :], dist[:, :, :], ALU.mult).then_inc(dist2_ready, 1)
                if works(i, 0):
                    pool.wait_ge(h_var_ready, a + 1)
                    if started(a):
                        pool.wait_ge(h_n_ready, a)
                    pool.tensor_tensor(h_rstd[:, :], h_var[:, :], half_power[:, :], ALU.pow).then_inc(h_rstd_ready, 1)
                    pool.wait_ge(h_n_ready, a + 1)
                    if started(a):
                        pool.wait_ge(stage_a_done, a)
                    pool.tensor_tensor(h_s[:, :, :], h_n[:, :, :].rearrange("p (j h) d -> p j (h d)", h=NH),
                                       head_scale[:, :].unsqueeze(1).to_broadcast([P, TPG, D]),
                                       ALU.mult).then_inc(h_s_ready, 1)
                    pool.wait_ge(h_s_ready, a + 1)
                    pool.tensor_tensor(x_all[:, a, :, :], x_all[:, a, :, :], h_s[:, :, :], ALU.add)\
                        .then_inc(stage_a_done, 1)

            pool.wait_ge(weights_ready, 1)
            steps(pool, step)

        @block.scalar
        def _(act):
            def copy(dst, src):
                return act.copy(dst, src)

            def step(i):
                a, b, c, d = i, i - 1, i - 2, i - 3
                if works(i, 3):
                    act.wait_ge(x4_in_psum, d + 1)
                    if started(d):
                        act.wait_ge(diff_ready, d)
                        act.wait_ge(x_r_ready, d)
                        act.wait_ge(x_k_ready, d)
                    copy(x_pad[:, :, 1:S + 1], bank[7][:, :].rearrange("p (n s) -> p n s", s=S)).then_inc(x4_ready, 1)
                if works(i, 2):
                    act.wait_ge(c_in_psum, c + 1)
                    if started(c):
                        act.wait_ge(win_scores_in_psum, c)
                    copy(c_t[:, :], bank[5][:, :]).then_inc(c_t_ready, 1)
                if works(i, 0):
                    act.wait_ge(q_in_psum, a + 1)
                    if started(a):
                        act.wait_ge(head_scores_done, NH * a)
                    copy(q_t[:, :], bank_q[:, :]).then_inc(q_t_ready, 1)
                    act.wait_ge(ctx_in_psum, a + 1)
                    copy(ctx_t[:, :], bank_ctx[:, :]).then_inc(ctx_t_ready, 1)
                if works(i, 2):
                    act.wait_ge(hid_in_psum, c + 1)
                    if started(c):
                        act.wait_ge(z_in_psum, c)
                    act.activation(hid[:, :], bank[6][0:HID, :], ACT.Tanh).then_inc(hid_ready, 1)
                if works(i, 0):
                    act.wait_ge(kw_in_psum, a + 1)
                    copy(kw_all[:, a, :], bank_q[:, :]).then_inc(kw_ready, 1)
                    act.wait_ge(neg_abs_ready, a + 1)
                    if started(a):
                        act.wait_ge(gate_z_ready, a)
                    act.activation(gate_u[:, :], neg_abs[:, :], ACT.Exp).then_inc(gate_u_ready, 1)
                if works(i, 1):
                    act.wait_ge(x_q_in_psum, b + 1)
                    if started(b):
                        act.wait_ge(ffn_in_psum, b)
                    copy(x_q_t[:, :], xq_ps).then_inc(x_q_t_ready, 1)
                if works(i, 2):
                    act.wait_ge(z_in_psum, c + 1)
                    if started(c):
                        act.wait_ge(pos_ready, c)
                    act.activation(tanh_z[:, :], z_ps, ACT.Tanh, scale=0.5).then_inc(tanh_z_ready, 1)
                if works(i, 3):
                    act.wait_ge(k_in_psum, d + 1)
                    if started(d):
                        act.wait_ge(k_act_ready, d)
                    act.activation(k_relu[:, :], bank[7][:, :], ACT.Relu).then_inc(k_relu_ready, 1)
                if works(i, 2):
                    act.wait_ge(dist2_ready, c + 1)
                    if started(c):
                        act.wait_ge(pg_ready, c)
                    act.activation(gauss[:, :, :], dist2[:, :, :], ACT.Exp, scale=-0.5).then_inc(gauss_ready, 1)
                if works(i, 0):
                    act.wait_ge(max_log_ready, a + 1)
                    if started(a):
                        act.wait_ge(heads_in_psum, a)
                    act.activation(exp_row[:, :], max_log[:, :], ACT.Exp, scale=-1.0).then_inc(exp_row_ready, 1)
                    for k in range(2):
                        act.wait_ge(decay_log_in_psum, 2 * a + k + 1)
                        if started(a):
                            act.wait_ge(weights_ready_a, 2 * a - 1 + k)
                        act.activation(decay[:, k, :, :, :], decay_ps[k], ACT.Exp).then_inc(decay_ready, 1)
                if works(i, 3):
                    act.wait_ge(r_in_psum, d + 1)
                    if started(d):
                        act.wait_ge(y_ready, d)
                    act.activation(r_tanh[:, :], bank[7][:, :], ACT.Tanh, scale=0.5).then_inc(r_tanh_ready, 1)
                if works(i, 2):
                    act.wait_ge(scs_ready, c + 1)
                    if started(c):
                        act.wait_ge(pg_ready, c)
                    act.activation(prob[:, :, :], scs[:, :, :], ACT.Exp).then_inc(prob_ready, 1)
                if works(i, 0):
                    act.wait_ge(heads_in_psum, a + 1)
                    if started(a):
                        act.wait_ge(h_ss_ready, a)
                    act.activation(h_sq[:, :, :].rearrange("p (k c) d -> p k c d", k=2), heads_ps[:, :, :, 0:DH],
                                   ACT.Square).then_inc(h_sq_ready, 1)
                if works(i, 2):
                    act.wait_ge(att_in_psum, c + 1)
                    if started(c):
                        act.wait_ge(win_in_psum, c)
                    copy(att_t[:, :, :], att_ps).then_inc(att_t_ready, 1)

            act.wait_ge(consts_ready, 1)
            steps(act, step)

        @block.vector
        def _(dve):
            done = [0]

            def then(instruction):
                done[0] += 1
                instruction.then_inc(split_step, 1)
                dve.wait_ge(split_step, done[0])

            dve.wait_ge(small_loaded, 16 * NSMALL)
            then(dve.memset(gate_w_q[:, :], 0.0))
            then(dve.memset(gate_w_c[:, :], 0.0))
            for h in range(NH):
                then(dve.memset(gate_w_c[DH * h:DH * h + DH, 2 * NH + h:2 * NH + h + 1], 1.0 / DH))
            for n, g in ((0, igk), (NH, fgk)):
                then(dve.tensor_copy(gate_w_q[:, n:n + NH], g[:, 0, :]))
                then(dve.tensor_tensor(gate_w_c[:, n:n + NH], g[:, 1, :], g[:, 2, :], ALU.add))
            then(dve.reciprocal(in_scale_inv[:, :], in_scale[:, :]))
            for n in range(NW):
                dve.wait_ge(w_transposed, n + 1)
                w_rows = HID if n == WP else D
                then(dve.tensor_copy(w_t[:, n, 0:w_rows], bank[n][:, 0:w_rows]))
            then(dve.tensor_scalar(w_rest[:, 0, :], w_t[:, WF, :], w_scale[:, 0:1], in_scale[:, 0:1], ALU.mult, ALU.mult))
            then(dve.tensor_copy(w_parts[:, 0, :], w_rest[:, 0, :]))
            then(dve.tensor_tensor(w_rest[:, 1, :], w_rest[:, 0, :], w_parts[:, 0, :], ALU.subtract))
            then(dve.tensor_copy(w_parts[:, 1, :], w_rest[:, 1, :]))
            then(dve.tensor_tensor(w_rest[:, 0, :], w_rest[:, 1, :], w_parts[:, 1, :], ALU.subtract))
            then(dve.tensor_copy(w_parts[:, 2, :], w_rest[:, 0, :]))
            dve.wait_ge(bias_loaded, 16 * 3)
            then(dve.tensor_copy(bias_tmp[64:128, 0, :], bias_rows[64:128, :]))
            then(dve.tensor_tensor(bias_rows[64:128, :], bias_rows[64:128, :], bias_tmp[64:128, 0, :], ALU.subtract))
            then(dve.tensor_copy(bias_tmp[96:128, 1, :], bias_rows[96:128, :]))
            then(dve.tensor_tensor(bias_rows[96:128, :], bias_rows[96:128, :], bias_tmp[96:128, 1, :], ALU.subtract))
            dve.tensor_copy(bias_parts[:, :, :], bias_rows[:, :].unsqueeze(1).to_broadcast([P, TPG, D]))\
                .then_inc(weights_ready, 1)
            dve.wait_ge(consts_ready, 1)

            def take_wait(dve):
                dve.memset(spare[:, :], 0.0)

            def norm_stats(st, g, ready, count):
                dve.wait_ge(ready, count)
                if started(g):
                    dve.wait_ge(mean_ready[st], 4 * g)
                for j in range(TPG):
                    dve.bn_stats(stats[st][:, j, :], x_all[:, g, j, :]).then_inc(stats_done[st], 1)
                if started(g):
                    dve.wait_ge(normed_ready[st], 4 * g)
                dve.wait_ge(stats_done[st], 4 * g + 4)
                take_wait(dve)
                for j in range(TPG):
                    dve.bn_aggr(mv[st][:, j, :], stats[st][:, j, :]).then_inc(mean_ready[st], 1)

            def norm_apply(st, g, scale, scale_ready, used):
                dve.wait_ge(scale_ready, g + 1)
                if started(g):
                    dve.wait_ge(used, g)
                for j in range(TPG):
                    dve.tensor_scalar(normed[st][:, j, :], x_all[:, g, j, :], mv[st][:, j, 0:1], scale[:, j:j + 1],
                                      ALU.subtract, ALU.mult).then_inc(normed_ready[st], 1)

            def step(i):
                a, b, c, d = i, i - 1, i - 2, i - 3
                if works(i, 3):
                    norm_stats(D_, d, stage_c_done, d + 1)
                if works(i, 2):
                    norm_stats(C_, c, stage_b_done, c + 1)
                if works(i, 1):
                    norm_stats(B_, b, stage_a_done, b + 1)
                if works(i, 0):
                    norm_stats(A_, a, x_loaded, 16 * (a + 1))
                if works(i, 3):
                    norm_apply(D_, d, rstd[D_], rstd_ready[D_], x4_in_psum)
                if works(i, 2):
                    norm_apply(C_, c, rstd[C_], rstd_ready[C_], c_in_psum)
                if works(i, 1):
                    norm_apply(B_, b, scale_b, scale_b_ready, clipped_ready)
                if works(i, 0):
                    norm_apply(A_, a, rstd[A_], rstd_ready[A_], q_in_psum)
                if works(i, 1):
                    dve.wait_ge(normed_ready[B_], 4 * b + 4)
                    if started(b):
                        dve.wait_ge(shifted_ready, b)
                    dve.tensor_scalar(clipped[:, :], normed[B_][:, :, :].rearrange("p j d -> p (j d)"), FP8_MAX,
                                      -FP8_MAX, ALU.min, ALU.max).then_inc(clipped_ready, 1)
                    dve.wait_ge(clipped_ready, b + 1)
                    if started(b):
                        dve.wait_ge(magic_ready, b)
                    dve.tensor_scalar(expo[:, :].bitcast(U32), clipped[:, :].bitcast(U32), 0x7F800000, None,
                                      ALU.bitwise_and).then_inc(expo_ready, 1)
                    dve.wait_ge(expo_ready, b + 1)
                    if started(b):
                        dve.wait_ge(x_q_ready, b)
                    dve.tensor_scalar(magic[:, :], expo[:, :], E4M3_MIN_NORMAL, ROUND_E4M3, ALU.max, ALU.mult)\
                        .then_inc(magic_ready, 1)
                    dve.wait_ge(magic_ready, b + 1)
                    if started(b):
                        dve.wait_ge(x_q_ready, b)
                    dve.tensor_tensor(shifted[:, :], clipped[:, :], magic[:, :], ALU.add).then_inc(shifted_ready, 1)
                    dve.wait_ge(shifted_ready, b + 1)
                    if started(b):
                        dve.wait_ge(x_q_in_psum, b)
                    dve.tensor_tensor(x_q[:, :, :].rearrange("p j d -> p (j d)"), shifted[:, :], magic[:, :],
                                      ALU.subtract).then_inc(x_q_ready, 1)
                if works(i, 0):
                    gate_steps(a)
                if works(i, 3):
                    for n, (dst, ready, used) in enumerate(((x_r, x_r_ready, r_in_psum), (x_k, x_k_ready, k_in_psum))):
                        dve.wait_ge(diff_ready, d + 1)
                        if started(d):
                            dve.wait_ge(used, d)
                        dve.scalar_tensor_tensor(out=dst[:, :, :], in0=diff[:, :, :], scalar=mu[:, n:n + 1],
                                                 in1=x_pad[:, :, 0:S], op0=ALU.mult, op1=ALU.add).then_inc(ready, 1)
                if works(i, 1):
                    dve.wait_ge(ffn_in_psum, b + 1)
                    dve.tensor_tensor(x_all[:, b, :, :], bank[4][:, :].rearrange("p (j d) -> p j d", j=TPG),
                                      x_all[:, b, :, :], ALU.add).then_inc(stage_b_done, 1)
                if works(i, 2):
                    window_steps(c)
                if works(i, 0):
                    row_steps(a)
                if works(i, 2):
                    softmax_steps(c)
                if works(i, 0):
                    for k in range(2):
                        dve.wait_ge(head_scores_done, NH * a + NH - 1 + k)
                        dve.wait_ge(decay_ready, 2 * a + k + 1)
                        if started(a):
                            dve.wait_ge(heads_in_psum, a)
                        dve.scalar_tensor_tensor(
                            out=weights[:, k, :, :, :].rearrange("p u j s -> p (u j s)"), in0=bank[k][:, :],
                            scalar=float(DH) ** -0.5, in1=decay[:, k, :, :, :].rearrange("p u j s -> p (u j s)"),
                            op0=ALU.mult, op1=ALU.mult).then_inc(weights_ready_a, 1)
                if works(i, 2):
                    late_softmax(c)
                if works(i, 3):
                    dve.wait_ge(v_in_psum, d + 1)
                    dve.wait_ge(r_tanh_ready, d + 1)
                    if started(d):
                        dve.wait_ge(stage_d_done, d)
                    dve.scalar_tensor_tensor(out=y[:, :], in0=r_tanh[:, :], scalar=1.0, in1=bank[7][:, :],
                                             op0=ALU.add, op1=ALU.mult).then_inc(y_ready, 1)
                    dve.wait_ge(y_ready, d + 1)
                    xd = x_all[:, d, :, :].rearrange("p j d -> p (j d)")
                    dve.scalar_tensor_tensor(out=xd, in0=y[:, :], scalar=0.5, in1=xd, op0=ALU.mult,
                                             op1=ALU.add).then_inc(stage_d_done, 1)
                if works(i, 0):
                    head_steps(a)
                if works(i, 2):
                    dve.wait_ge(win_in_psum, c + 1)
                    dve.tensor_tensor(x_all[:, c, :, :], bank[5][:, :].rearrange("p (j d) -> p j d", j=TPG),
                                      x_all[:, c, :, :], ALU.add).then_inc(stage_c_done, 1)

            def gate_steps(a):
                fg = gates[:, 1, :, :].rearrange("p j h -> p (j h)")
                dve.wait_ge(gates_in_psum, a + 1)
                if started(a):
                    dve.wait_ge(gates_exp_ready, a)
                for k in range(2):
                    dve.tensor_tensor(gates[:, k, :, :], gates_ps[:, :, NH * k:NH * k + NH],
                                      gate_bias[:, NH * k:NH * k + NH].unsqueeze(1).to_broadcast([P, TPG, NH]),
                                      ALU.add).then_inc(gates_ready, 1)
                if started(a):
                    dve.wait_ge(v_aug_ready, a)
                dve.tensor_copy(v_mean[:, :].rearrange("p (j h) -> p j h", h=NH), gates_ps[:, :, 2 * NH:3 * NH])\
                    .then_inc(v_mean_ready, 1)
                dve.wait_ge(gates_ready, 2 * a + 2)
                if started(a):
                    dve.wait_ge(gate_u_ready, a)
                dve.scalar_tensor_tensor(out=neg_abs[:, :], in0=fg, scalar=-1.0, in1=fg, op0=ALU.mult, op1=ALU.min)\
                    .then_inc(neg_abs_ready, 1)
                if started(a):
                    dve.wait_ge(log_f_ready, a)
                dve.tensor_scalar(low[:, :], fg, 0.0, None, ALU.min).then_inc(low_ready, 1)
                dve.wait_ge(gate_u_ready, a + 1)
                dve.tensor_scalar(gate_den[:, :], gate_u[:, :], 2.0, None, ALU.add).then_inc(gate_den_ready, 1)
                dve.wait_ge(gate_den_ready, a + 1)
                dve.reciprocal(gate_rec[:, :], gate_den[:, :]).then_inc(gate_rec_ready, 1)
                dve.wait_ge(gate_rec_ready, a + 1)
                dve.tensor_tensor(gate_z[:, :], gate_u[:, :], gate_rec[:, :], ALU.mult).then_inc(gate_z_ready, 1)
                dve.wait_ge(gate_z_ready, a + 1)
                dve.tensor_tensor(gate_z2[:, :], gate_z[:, :], gate_z[:, :], ALU.mult).then_inc(gate_z2_ready, 1)
                dve.wait_ge(gate_z2_ready, a + 1)
                dve.tensor_scalar(gate_q[0][:, :], gate_z2[:, :], ATANH[4], None, ALU.mult).then_inc(gate_q0, 1)
                for n, (before, after) in enumerate(((gate_q0, gate_q1), (gate_q1, gate_q2), (gate_q2, gate_q3))):
                    dve.wait_ge(before, a + 1)
                    dve.scalar_tensor_tensor(out=gate_q[n + 1][:, :], in0=gate_q[n][:, :], scalar=ATANH[3 - n],
                                             in1=gate_z2[:, :], op0=ALU.add, op1=ALU.mult).then_inc(after, 1)
                dve.wait_ge(gate_q3, a + 1)
                dve.scalar_tensor_tensor(out=gate_q[4][:, :], in0=gate_q[3][:, :], scalar=ATANH[0], in1=gate_z[:, :],
                                         op0=ALU.add, op1=ALU.mult).then_inc(gate_q4, 1)
                dve.wait_ge(gate_q4, a + 1)
                dve.wait_ge(low_ready, a + 1)
                dve.scalar_tensor_tensor(out=fg, in0=gate_q[4][:, :], scalar=-2.0, in1=low[:, :], op0=ALU.mult,
                                         op1=ALU.add).then_inc(log_f_ready, 1)
                dve.wait_ge(log_f_ready, a + 1)
                if started(a):
                    dve.wait_ge(rows_in_psum, a)
                dve.tensor_tensor(gates_exp[:, :, :, :],
                                  gates[:, :, :, :].rearrange("p k j h -> p k (j h)").unsqueeze(2).to_broadcast([P, 2, 8, 16]),
                                  batch_mask[:, :, :].rearrange("p r b -> p (r b)").unsqueeze(1).unsqueeze(3)
                                  .to_broadcast([P, 2, 8, 16]), ALU.mult).then_inc(gates_exp_ready, 1)

            def row_steps(a):
                dve.wait_ge(rows_in_psum, a + 1)
                if started(a):
                    dve.wait_ge(rest_ready, 2 * a)
                    dve.wait_ge(run_max_ready, a)
                dve.tensor_copy(a_row[:, :], rows_ps[:, 1, :]).then_inc(a_row_ready, 1)
                dve.wait_ge(a_row_ready, a + 1)
                if started(a):
                    dve.wait_ge(parts_ready, a)
                    dve.wait_ge(sum_row_ready, a)
                dve.tensor_tensor_scan(run_max[:, :], a_row[:, :], a_row[:, :], -3.0e38, ALU.max, ALU.max)\
                    .then_inc(run_max_ready, 1)
                dve.tensor_tensor(rest[:, 0:2, :], a_row[:, :].unsqueeze(1).to_broadcast([P, 2, S]),
                                  row_mask[:, :].unsqueeze(2).to_broadcast([P, 2, S]), ALU.mult)\
                    .then_inc(rest_ready, 1)
                dve.wait_ge(run_max_ready, a + 1)
                dve.tensor_scalar(rest[:, 2, :], run_max[:, :], -1.0, None, ALU.mult).then_inc(rest_ready, 1)
                if started(a):
                    dve.wait_ge(exp_row_ready, a)
                dve.tensor_tensor(max_log[:, :], rows_ps[:, 0, :], run_max[:, :], ALU.add).then_inc(sum_row_ready, 1)
                dve.wait_ge(sum_row_ready, a + 1)
                dve.tensor_scalar(max_log[:, :], max_log[:, :], MIN_LOG, None, ALU.max).then_inc(max_log_ready, 1)
                dve.wait_ge(rest_ready, 2 * a + 2)
                dve.tensor_copy(part_tmp[64:128, 0, :, :], rest[64:128, :, :]).then_inc(part0_ready, 1)
                dve.wait_ge(part0_ready, a + 1)
                dve.tensor_tensor(rest[64:128, :, :], rest[64:128, :, :], part_tmp[64:128, 0, :, :], ALU.subtract)\
                    .then_inc(rest1_ready, 1)
                dve.wait_ge(rest1_ready, a + 1)
                dve.tensor_copy(part_tmp[96:128, 1, :, :], rest[96:128, :, :]).then_inc(part1_ready, 1)
                dve.wait_ge(part1_ready, a + 1)
                dve.tensor_tensor(rest[96:128, :, :], rest[96:128, :, :], part_tmp[96:128, 1, :, :], ALU.subtract)\
                    .then_inc(rest2_ready, 1)
                dve.wait_ge(rest2_ready, a + 1)
                if started(a):
                    dve.wait_ge(decay_log_in_psum, 2 * a)
                dve.tensor_copy(parts[:, :, :], rest[:, :, :]).then_inc(parts_ready, 1)

            def head_steps(a):
                dve.wait_ge(h_sq_ready, a + 1)
                if started(a):
                    dve.wait_ge(norm_n_ready, a)
                dve.tensor_copy(floor_n[:, :], exp_col_ps).then_inc(floor_n_ready, 1)
                dve.wait_ge(floor_n_ready, 2 * a + 1)
                if started(a):
                    dve.wait_ge(norm_e_ready, a)
                sums = heads_ps[:, :, :, DH]
                floor_v = floor_n[:, :].rearrange("p (k c) -> p k c", k=2)
                norm_v = norm_n[:, :].rearrange("p (k c) -> p k c", k=2)
                dve.scalar_tensor_tensor(out=floor_v, in0=sums, scalar=-1.0, in1=floor_v, op0=ALU.mult, op1=ALU.max)\
                    .then_inc(floor_n_ready, 1)
                dve.wait_ge(floor_n_ready, 2 * a + 2)
                dve.tensor_tensor(norm_v, sums, floor_v, ALU.max).then_inc(norm_n_ready, 1)
                dve.wait_ge(norm_n_ready, a + 1)
                if started(a):
                    dve.wait_ge(norm_q_ready, a)
                dve.tensor_scalar(norm_e[:, :], norm_n[:, :], EPS_BACKEND, None, ALU.add).then_inc(norm_e_ready, 1)
                dve.wait_ge(norm_e_ready, a + 1)
                if started(a):
                    dve.wait_ge(h_var_ready, a)
                dve.scalar_tensor_tensor(out=norm_q[:, :], in0=norm_e[:, :], scalar=EPS_HEAD, in1=norm_e[:, :],
                                         op0=ALU.mult, op1=ALU.mult).then_inc(norm_q_ready, 1)
                dve.tensor_reduce(h_ss[:, :], h_sq[:, :, :], AX_X, ALU.add).then_inc(h_ss_ready, 1)
                dve.wait_ge(h_ss_ready, a + 1)
                dve.wait_ge(norm_q_ready, a + 1)
                if started(a):
                    dve.wait_ge(h_rstd_ready, a)
                dve.scalar_tensor_tensor(out=h_var[:, :], in0=h_ss[:, :], scalar=1.0 / DH, in1=norm_q[:, :],
                                         op0=ALU.mult, op1=ALU.add).then_inc(h_var_ready, 1)
                dve.wait_ge(h_rstd_ready, a + 1)
                if started(a):
                    dve.wait_ge(h_s_ready, a)
                dve.tensor_tensor(h_n[:, :, :].rearrange("p (k c) d -> p k c d", k=2), heads_ps[:, :, :, 0:DH],
                                  h_rstd[:, :].rearrange("p (k c) -> p k c", k=2).unsqueeze(3)
                                  .to_broadcast([P, 2, 8, DH]), ALU.mult).then_inc(h_n_ready, 1)

            def window_steps(c):
                dve.wait_ge(tanh_z_ready, c + 1)
                if started(c):
                    dve.wait_ge(dist_ready, c)
                    dve.wait_ge(pos_gt_ready, c)
                dve.tensor_scalar(pos[:, :], tanh_z[:, :], S / 2.0, S / 2.0, ALU.mult, ALU.add).then_inc(pos_ready, 1)
                dve.wait_ge(pos_ready, c + 1)
                dve.tensor_scalar(pos_r[:, :], pos[:, :], ROUND_INT, -ROUND_INT, ALU.add, ALU.add).then_inc(pos_r_ready, 1)
                dve.wait_ge(pos_r_ready, c + 1)
                dve.tensor_tensor(pos_gt[:, :], pos_r[:, :], pos[:, :], ALU.is_gt).then_inc(pos_gt_ready, 1)
                dve.wait_ge(pos_gt_ready, c + 1)
                dve.tensor_tensor(pos_fl[:, :], pos_r[:, :], pos_gt[:, :], ALU.subtract).then_inc(pos_fl_ready, 1)
                dve.wait_ge(pos_fl_ready, c + 1)
                if started(c):
                    dve.wait_ge(edges_ready, c)
                dve.tensor_scalar(edge[:, :, 0], pos_fl[:, :], -1.0, 3.0, ALU.mult, ALU.add).then_inc(edge_ready, 1)
                dve.tensor_scalar(edge[:, :, 1], pos_fl[:, :], 3.0 - S, None, ALU.add).then_inc(edge_ready, 1)
                if started(c):
                    dve.wait_ge(off_sq_ready, c)
                dve.tensor_tensor(off[:, :, :], iota[:, :].unsqueeze(1).to_broadcast([P, TPG, S]),
                                  pos_fl[:, :].unsqueeze(2).to_broadcast([P, TPG, S]), ALU.subtract).then_inc(off_ready, 1)
                dve.wait_ge(off_ready, c + 1)
                if started(c):
                    dve.wait_ge(outside_ready, c)
                dve.scalar_tensor_tensor(out=off_sq[:, :, :], in0=off[:, :, :], scalar=1.0, in1=off[:, :, :],
                                         op0=ALU.add, op1=ALU.mult).then_inc(off_sq_ready, 1)
                dve.wait_ge(off_sq_ready, c + 1)
                if started(c):
                    dve.wait_ge(scm_ready, c)
                dve.tensor_scalar(outside[:, :, :], off_sq[:, :, :], 4.0, -BIG, ALU.is_ge, ALU.mult)\
                    .then_inc(outside_ready, 1)

            def softmax_steps(c):
                dve.wait_ge(win_scores_in_psum, c + 1)
                dve.wait_ge(outside_ready, c + 1)
                if started(c):
                    dve.wait_ge(scs_ready, c)
                dve.tensor_tensor(scm[:, :, :], win_ps, outside[:, :, :], ALU.add).then_inc(scm_ready, 1)
                dve.wait_ge(scm_ready, c + 1)
                dve.tensor_reduce(sc_max[:, :], scm[:, :, :], AX_X, ALU.max).then_inc(sc_max_ready, 1)
                dve.wait_ge(sc_max_ready, c + 1)
                if started(c):
                    dve.wait_ge(prob_ready, c)
                dve.tensor_tensor(scs[:, :, :], scm[:, :, :], sc_max[:, :].unsqueeze(2).to_broadcast([P, TPG, S]),
                                  ALU.subtract).then_inc(scs_ready, 1)

            def late_softmax(c):
                ends = prob[:, :, 0:S:S - 1]
                dve.wait_ge(prob_ready, c + 1)
                dve.wait_ge(edge_ready, 2 * c + 2)
                dve.scalar_tensor_tensor(out=ends, in0=edge[:, :, :], scalar=1.0, in1=ends, op0=ALU.max,
                                         op1=ALU.mult).then_inc(edges_ready, 1)
                dve.wait_ge(edges_ready, c + 1)
                if started(c):
                    dve.wait_ge(rden_ready, c)
                dve.tensor_reduce(den[:, :], prob[:, :, :], AX_X, ALU.add).then_inc(den_ready, 1)
                dve.wait_ge(den_ready, c + 1)
                if started(c):
                    dve.wait_ge(att_ready, c)
                dve.reciprocal(rden[:, :], den[:, :]).then_inc(rden_ready, 1)
                dve.wait_ge(gauss_ready, c + 1)
                dve.tensor_tensor(pg[:, :, :], prob[:, :, :], gauss[:, :, :], ALU.mult).then_inc(pg_ready, 1)
                dve.wait_ge(pg_ready, c + 1)
                dve.wait_ge(rden_ready, c + 1)
                if started(c):
                    dve.wait_ge(att_in_psum, c)
                dve.tensor_tensor(att[:, :, :], pg[:, :, :], rden[:, :].unsqueeze(2).to_broadcast([P, TPG, S]),
                                  ALU.mult).then_inc(att_ready, 1)

            steps(dve, step)

        @block.tensor
        def _(pe):
            pe.wait_ge(ident_ready, 1)
            pe.wait_ge(w_loaded, 16 * NW)
            for n in range(NW):
                rows = HID if n == WP else D
                pe.transpose(bank[n][:, 0:rows], w_raw[0:rows, n, :], ident[0:rows, 0:rows]).then_inc(w_transposed, 1)
            pe.wait_ge(weights_ready, 1)
            pe.wait_ge(consts_ready, 1)

            def take_wait():
                pe.matmul(bank[6][0:32, 508:510], ident_bf[:, 0:32], ident_bf[:, 0:2], start=True, stop=True)

            def halves(j=None):
                for b in range(2):
                    yield b, slice(S * b, S * b + S)

            def step(i):
                a, b, c, d = i, i - 1, i - 2, i - 3
                if works(i, 3):
                    pe.wait_ge(normed_ready[D_], 4 * d + 4)
                    if started(d):
                        pe.wait_ge(y_ready, d)
                    for j in range(TPG):
                        last = pe.transpose(bank[7][:, P * j:P * j + P], normed[D_][:, j, :], ident[:, :])
                    last.then_inc(x4_in_psum, 1)
                if works(i, 2):
                    pe.wait_ge(normed_ready[C_], 4 * c + 4)
                    if started(c):
                        pe.wait_ge(stage_c_done, c)
                    for j in range(TPG):
                        last = pe.transpose(bank[5][:, P * j:P * j + P], normed[C_][:, j, :], ident[:, :])
                    last.then_inc(c_in_psum, 1)
                if works(i, 0):
                    pe.wait_ge(normed_ready[A_], 4 * a + 4)
                    if started(a):
                        pe.wait_ge(weights_ready_a, 2 * a)
                    for j in range(TPG):
                        last = pe.transpose(bank_q[:, P * j:P * j + P], normed[A_][:, j, :], ident[:, :])
                    last.then_inc(q_in_psum, 1)
                    pe.wait_ge(ctx_a_loaded, 16 * (a + 1))
                    for j in range(TPG):
                        last = pe.transpose(bank_ctx[:, P * j:P * j + P], ctx_a[:, j, :], ident[:, :])
                    last.then_inc(ctx_in_psum, 1)
                if works(i, 2):
                    pe.wait_ge(c_t_ready, c + 1)
                    if started(c):
                        pe.wait_ge(att_t_ready, c)
                    pe.matmul(bank[6][0:HID, :], w_t[:, WP, 0:HID], c_t[:, :], start=True, stop=True)\
                        .then_inc(hid_in_psum, 1)
                if works(i, 0):
                    pe.wait_ge(q_t_ready, a + 1)
                    pe.wait_ge(ctx_t_ready, a + 1)
                    if started(a):
                        pe.wait_ge(h_n_ready, a)
                    for j in range(TPG):
                        pe.matmul(gates_ps[:, j, :], q_t[:, P * j:P * j + P], gate_w_q[:, :], start=True, stop=False)
                        last = pe.matmul(gates_ps[:, j, :], ctx_t[:, P * j:P * j + P], gate_w_c[:, :],
                                         start=False, stop=True)
                    last.then_inc(gates_in_psum, 1)
                    pe.matmul(bank_q[:, :], w_t[:, WA, :], ctx_t[:, :], start=True, stop=True).then_inc(kw_in_psum, 1)
                if works(i, 1):
                    pe.wait_ge(x_q_ready, b + 1)
                    if started(b):
                        pe.wait_ge(stage_b_done, b)
                    for j in range(TPG):
                        last = pe.transpose(xq_ps[:, P * j:P * j + P], x_q[:, j, :], ident_bf[:, :])
                    last.then_inc(x_q_in_psum, 1)
                if works(i, 2):
                    pe.wait_ge(hid_ready, c + 1)
                    for j in range(TPG):
                        last = pe.matmul(z_ps[:, j:j + 1], hid[:, P * j:P * j + P], vp_col[:, :], start=True, stop=True)
                    last.then_inc(z_in_psum, 1)
                if works(i, 3):
                    pe.wait_ge(x_k_ready, d + 1)
                    pe.matmul(bank[7][:, :], w_t[:, WK, :], x_k[:, :, :], start=True, stop=True).then_inc(k_in_psum, 1)
                if works(i, 2):
                    pe.wait_ge(kw_c_ready, c + 1)
                    pe.wait_ge(tanh_z_ready, c + 1)
                    for j in range(TPG):
                        for h, half in halves():
                            cols = slice(P * j + S * h, P * j + S * h + S)
                            last = pe.matmul(win_ps[half, j, :], c_t[:, cols], kw_c[:, cols], start=True, stop=True)
                    last.then_inc(win_scores_in_psum, 1)
                if works(i, 1):
                    pe.wait_ge(x_q_t_ready, b + 1)
                    pe.matmul(ffn_ps[:, :], ones_bf[:, :], bias_parts[:, :, :], start=True, stop=False)
                    for j in range(TPG):
                        for n in range(3):
                            last = pe.matmul(ffn_ps[:, P * j:P * j + P], x_q_t[:, P * j:P * j + P], w_parts[:, n, :],
                                             start=False, stop=(n == 2 and j == TPG - 1))
                    last.then_inc(ffn_in_psum, 1)
                if works(i, 0):
                    pe.wait_ge(gates_exp_ready, a + 1)
                    ig = gates_exp[:, 0, :, :].rearrange("p r c -> p (r c)")
                    fg = gates_exp[:, 1, :, :].rearrange("p r c -> p (r c)")
                    pe.matmul(rows_ps[:, 0, :], fg, cum[:, :], start=True, stop=True)
                    pe.matmul(rows_ps[:, 1, :], ig, pick[:, :], start=True, stop=False)
                    pe.matmul(rows_ps[:, 1, :], fg, neg_cum[:, :], start=False, stop=True).then_inc(rows_in_psum, 1)
                    pe.wait_ge(kw_ready, a + 1)
                    for h in range(NH):
                        hrows = slice(DH * h, DH * h + DH)
                        if h >= 2:
                            pe.wait_ge(head_scores_done, NH * a + h - 1)
                        for j in range(TPG):
                            for n, half in halves():
                                cols = slice(P * j + S * n, P * j + S * n + S)
                                last = pe.matmul(score_ps[h % 2][half, h // 2, j, :], ctx_t[hrows, cols],
                                                 q_t[hrows, cols], start=True, stop=True)
                        last.then_inc(head_scores_done, 1)
                if works(i, 3):
                    pe.wait_ge(k_relu_ready, d + 1)
                    pe.wait_ge(x_r_ready, d + 1)
                    xr = x_r[:, :, :].rearrange("p n s -> p (n s)")
                    for j in range(TPG):
                        last = pe.matmul(bank[7][:, P * j:P * j + P], xr[:, P * j:P * j + P], w_t[:, WR, :],
                                         start=True, stop=True)
                    last.then_inc(r_in_psum, 1)
                if works(i, 0):
                    pe.wait_ge(parts_ready, a + 1)
                    pe.wait_ge(max_log_ready, a + 1)
                    for k in range(2):
                        flat = bank[2 + k][:, :]
                        pe.matmul(flat, ident_bf[:, :], causal[:, :, :, :], start=True, stop=False)
                        pe.matmul(flat, parts[:, 0:2, :], row_cols[:, k, :, :, :], start=False, stop=False)
                        for u in range(2):
                            for j in range(TPG):
                                last = pe.matmul(decay_ps[k][:, u, j, :],
                                                 pick_row[:, NH * j + 2 * u + k, :, :], parts[:, 2, :],
                                                 start=False, stop=(u == 1 and j == TPG - 1))
                        last.then_inc(decay_log_in_psum, 1)
                if works(i, 3):
                    pe.wait_ge(k_act_ready, d + 1)
                    pe.wait_ge(r_tanh_ready, d + 1)
                    for j in range(TPG):
                        last = pe.matmul(bank[7][:, P * j:P * j + P], k_act[:, P * j:P * j + P], w_t[:, WV, :],
                                         start=True, stop=True)
                    last.then_inc(v_in_psum, 1)
                if works(i, 0):
                    pe.wait_ge(weights_ready_a, 2 * a + 2)
                    pe.wait_ge(v_aug_ready, a + 1)
                    pe.wait_ge(exp_row_ready, a + 1)
                    for n, half in halves():
                        pe.matmul(exp_col_ps[half, :], exp_row[0:32, :], back[:, n, :], start=True, stop=True)
                    for j in range(TPG):
                        for h in range(NH):
                            for n, half in halves():
                                last = pe.matmul(heads_ps[half, j // 2, NH * (j % 2) + h, :],
                                                 weights[half, h % 2, h // 2, j, :], v_aug[half, j, h, :],
                                                 start=True, stop=True)
                    last.then_inc(heads_in_psum, 1)
                if works(i, 2):
                    pe.wait_ge(att_ready, c + 1)
                    take_wait()
                    for j in range(TPG):
                        for n, half in halves():
                            last = pe.matmul(att_ps[half, j, :], att[half, j, :], ident[half, half], start=True, stop=True)
                    last.then_inc(att_in_psum, 1)
                    pe.wait_ge(att_t_ready, c + 1)
                    pe.wait_ge(ctx_c_loaded, 16 * (c + 1))
                    take_wait()
                    for j in range(TPG):
                        for n, half in halves():
                            last = pe.matmul(bank[5][half, P * j:P * j + P], att_t[half, j, :], ctx_c[half, j, :],
                                             start=True, stop=True)
                    last.then_inc(win_in_psum, 1)

            steps(pe, step)



_INS = ['x', 'ctx_1024', 'L0_xattn_igate_kernel', 'L0_xattn_igate_bias', 'L0_xattn_fgate_kernel',
        'L0_xattn_fgate_bias', 'L0_xattn_outnorm_scale', 'L0_ffn_weight_fp8', 'L0_ffn_bias', 'L0_ffn_input_scale',
        'L0_ffn_weight_scale', 'L1_xattn_W_a', 'L1_xattn_W_p', 'L1_xattn_V_p', 'L1_ffn_W_r', 'L1_ffn_W_k',
        'L1_ffn_W_v', 'L1_ffn_mu_r', 'L1_ffn_mu_k']


def kernel(**inputs):
    import numpy as _np
    import concourse.bacc as _bacc
    from concourse import mybir as _mybir
    from concourse.bass_utils import run_bass_kernel_spmd as _run

    nc = _bacc.Bacc("TRN2", target_bir_lowering=False, num_devices=1)
    arrays, args = {}, []
    for name in _INS:
        a = _np.ascontiguousarray(inputs[name])
        arrays[f"in_{name}_dram"] = a
        args.append(nc.dram_tensor(f"in_{name}_dram", a.shape, _mybir.dt.from_np(a.dtype), kind="ExternalInput").ap())
    out = nc.dram_tensor("out_0_dram", tuple(inputs["x"].shape), _mybir.dt.float32, kind="ExternalOutput").ap()
    xattn_ffn_two_layers(nc, *args, out)
    r = _run(nc, [arrays], core_ids=[0])
    return r.results[0]["out_0_dram"]
```

```python
from contextlib import ExitStack

import concourse.bass as bass
from concourse import mybir

ALU = mybir.AluOpType
ACT = mybir.ActivationFunctionType
F32 = mybir.dt.float32
BF16 = mybir.dt.bfloat16
U32 = mybir.dt.uint32
AX_X = mybir.AxisListType.X

P = 128
S = 64
D = 128
NH = 4
DH = D // NH
TPG = 4
GC = TPG * D
HID = 100
BIG = 1.0e30
EPS_NORM = 1e-5
EPS_HEAD = 1e-6
EPS_BACKEND = 1e-6
FP8_MAX = 448.0
ROUND_INT = 8388608.0
ROUND_E4M3 = 1.5 * 2.0**20
E4M3_MIN_NORMAL = 2.0**-6
ATANH = (1.0, 0.33333158, 0.20012427, 0.13980709, 0.14087329)
MIN_LOG = -34.0


def xattn_ffn_two_layers(
    nc, x, ctx, igate_kernel, igate_bias, fgate_kernel, fgate_bias, outnorm_scale,
    weight_fp8, ffn_bias, input_scale, weight_scale, W_a, W_p, V_p, W_r, W_k, W_v, mu_r, mu_k, out,
):
    B = x.shape[0]
    NT = B * S // P
    NG = NT // TPG
    LAST = 7
    STEADY = LAST + 1

    x_dram = x.rearrange("b s d -> (b s) d").rearrange("(g j p) d -> g p j d", j=TPG, p=P)
    ctx_dram = ctx.rearrange("b s d -> (b s) d").rearrange("(g j p) d -> g p j d", j=TPG, p=P)
    out_dram = out.rearrange("b s d -> (b s) d").rearrange("(g j p) d -> g p j d", j=TPG, p=P)

    with ExitStack() as stack:
        def sb(name, shape, dt=F32):
            return stack.enter_context(nc.sbuf_tensor(name, shape, dt))

        def sem(name):
            return stack.enter_context(nc.semaphore(name))

        banks = stack.enter_context(nc.psum_tensor("banks", [P, 8, 512], F32))
        bank = [banks[:, i, :] for i in range(8)]

        x_all = sb("x_all", [P, NG, TPG, D])
        kw_all = sb("kw_all", [P, NG, TPG * P])

        ident = sb("ident", [P, P])
        ident_bf = sb("ident_bf", [P, P], BF16)
        ones_bf = sb("ones_bf", [P, P], BF16)
        cum = sb("cum", [P, S])
        neg_cum = sb("neg_cum", [P, S])
        pick = sb("pick", [P, S])
        causal = sb("causal", [P, NH // 2, TPG, S], BF16)
        batch_mask = sb("batch_mask", [P, 4, 2])
        row_mask = sb("row_mask", [P, 2])
        pick_row = sb("pick_row", [P, 16, 2, S], BF16)
        row_cols = sb("row_cols", [P, 2, 2, TPG, S], BF16)
        back = sb("back", [32, 2, 16])
        iota = sb("iota", [P, S])
        eps_col = sb("eps_col", [P, 1])
        iota_half = sb("iota_half", [P, S])
        pick_of_row = sb("pick_of_row", [P, 16, 2])
        cols_of_row = sb("cols_of_row", [P, 2, 2, TPG])
        window_edge = sb("window_edge", [P, 1])
        spare_pool = sb("spare_pool", [P, 1])
        spare = sb("spare", [P, 4])
        spare_act = sb("spare_act", [P, 6])
        half_power = sb("half_power", [P, 16])

        NW = 6
        WA, WP, WR, WK, WV, WF = range(NW)
        w_raw = sb("w_raw", [P, NW, D])
        w_t = sb("w_t", [P, NW, D])
        vp_col = sb("vp_col", [HID, 1])
        igk = sb("igk", [P, 3, NH])
        fgk = sb("fgk", [P, 3, NH])
        gate_w_q = sb("gate_w_q", [P, 12])
        gate_w_c = sb("gate_w_c", [P, 12])
        gate_bias = sb("gate_bias", [P, 2 * NH])
        head_scale = sb("head_scale", [P, D])
        in_scale = sb("in_scale", [P, 1])
        w_scale = sb("w_scale", [P, 1])
        in_scale_inv = sb("in_scale_inv", [P, 1])
        mu = sb("mu", [P, 2])
        one_less_mu = sb("one_less_mu", [P, 2])
        w_rest = sb("w_rest", [P, 2, D])
        w_parts = sb("w_parts", [P, 3, D], BF16)
        bias_rows = sb("bias_rows", [P, D])
        bias_tmp = sb("bias_tmp", [P, 2, D], BF16)
        bias_parts = sb("bias_parts", [P, TPG, D], BF16)

        stats = [sb(f"stats_{s}", [P, TPG, 6]) for s in "abcd"]
        mv = [sb(f"mv_{s}", [P, TPG, 2]) for s in "abcd"]
        var_eps = [sb(f"var_eps_{s}", [P, TPG]) for s in "abcd"]
        rstd = [sb(f"rstd_{s}", [P, TPG]) for s in "abcd"]
        shift = [sb(f"shift_{s}", [P, TPG]) for s in "abcd"]
        normed = [sb(f"normed_{s}", [P, TPG, D]) for s in "abcd"]

        ctx_a = sb("ctx_a", [P, TPG, D])
        q_t = sb("q_t", [P, TPG * P])
        ctx_t = sb("ctx_t", [P, TPG * P])
        gates = sb("gates", [P, 2, TPG, NH])
        v_mean = sb("v_mean", [P, 16])
        neg_abs = sb("neg_abs", [P, 16])
        low = sb("low", [P, 16])
        gate_u = sb("gate_u", [P, 16])
        gate_den = sb("gate_den", [P, 16])
        gate_rec = sb("gate_rec", [P, 16])
        gate_z = sb("gate_z", [P, 16])
        gate_z2 = sb("gate_z2", [P, 16])
        gate_q = [sb(f"gate_q{k}", [P, 16]) for k in range(5)]
        gates_exp = sb("gates_exp", [P, 2, 8, 16])
        a_row = sb("a_row", [P, S])
        run_max = sb("run_max", [P, S])
        max_log = sb("max_log", [P, S])
        exp_row = sb("exp_row", [P, S])
        rest = sb("rest", [P, 3, S])
        part_tmp = sb("part_tmp", [P, 2, 3, S], BF16)
        parts = sb("parts", [P, 3, S], BF16)
        v_aug = sb("v_aug", [P, TPG, NH, DH + 1])
        decay = sb("decay", [P, 2, 2, TPG, S])
        weights = sb("weights", [P, 2, 2, TPG, S])
        h_sq = sb("h_sq", [P, 16, DH])
        h_ss = sb("h_ss", [P, 16])
        floor_n = sb("floor_n", [P, 16])
        norm_n = sb("norm_n", [P, 16])
        norm_e = sb("norm_e", [P, 16])
        norm_q = sb("norm_q", [P, 16])
        h_var = sb("h_var", [P, 16])
        h_rstd = sb("h_rstd", [P, 16])
        h_n = sb("h_n", [P, 16, DH])
        h_s = sb("h_s", [P, TPG, D])

        scale_b = sb("scale_b", [P, TPG])
        clipped = sb("clipped", [P, GC])
        expo = sb("expo", [P, GC])
        magic = sb("magic", [P, GC])
        shifted = sb("shifted", [P, GC])
        x_q = sb("x_q", [P, TPG, D], BF16)
        x_q_t = sb("x_q_t", [P, TPG * P], BF16)

        ctx_c = sb("ctx_c", [P, TPG, D])
        kw_c = sb("kw_c", [P, TPG * P])
        c_t = sb("c_t", [P, TPG * P])
        hid = sb("hid", [HID, TPG * P])
        tanh_z = sb("tanh_z", [P, TPG])
        pos = sb("pos", [P, TPG])
        pos_r = sb("pos_r", [P, TPG])
        pos_gt = sb("pos_gt", [P, TPG])
        pos_fl = sb("pos_fl", [P, TPG])
        edge = sb("edge", [P, TPG, 2])
        off = sb("off", [P, TPG, S])
        off_sq = sb("off_sq", [P, TPG, S])
        outside = sb("outside", [P, TPG, S])
        dist = sb("dist", [P, TPG, S])
        dist2 = sb("dist2", [P, TPG, S])
        gauss = sb("gauss", [P, TPG, S])
        scm = sb("scm", [P, TPG, S])
        neg_max = sb("neg_max", [P, TPG])
        prob = sb("prob", [P, TPG, S])
        den = sb("den", [P, TPG])
        rden = sb("rden", [P, TPG])
        pg = sb("pg", [P, TPG, S])
        att = sb("att", [P, TPG, S])
        att_t = sb("att_t", [P, TPG, S])

        NB = 2 * TPG
        x_now = sb("x_now", [P, GC])
        x_prev = sb("x_prev", [P, NB, S])
        w_mix = sb("w_mix", [P, 2, D])
        x_k = sb("x_k", [P, GC])
        k_relu = sb("k_relu", [P, GC])
        k_act = sb("k_act", [P, GC])
        r_tanh = sb("r_tanh", [P, GC])
        y = sb("y", [P, GC])

        x_loaded, ctx_a_loaded, ctx_c_loaded = sem("x_loaded"), sem("ctx_a_loaded"), sem("ctx_c_loaded")
        w_loaded, small_loaded, bias_loaded = sem("w_loaded"), sem("small_loaded"), sem("bias_loaded")
        ident_ready, consts_step, consts_ready = sem("ident_ready"), sem("consts_step"), sem("consts_ready")
        w_transposed, w_copied, gate_weights_ready = sem("w_transposed"), sem("w_copied"), sem("gate_weights_ready")
        consts_spread = sem("consts_spread")
        split_step, weights_ready, bias_cleared = sem("split_step"), sem("weights_ready"), sem("bias_cleared")
        stats_done = [sem(f"stats_{s}_done") for s in "abcd"]
        mean_ready = [sem(f"mean_{s}_ready") for s in "abcd"]
        eps_added = [sem(f"eps_{s}_added") for s in "abcd"]
        rstd_ready = [sem(f"rstd_{s}_ready") for s in "abcd"]
        shift_ready = [sem(f"shift_{s}_ready") for s in "abcd"]
        normed_ready = [sem(f"normed_{s}_ready") for s in "abcd"]
        (
            q_in_psum, weighted, ctx_in_psum, head_scores_done, q_t_ready, ctx_t_ready, gates_in_psum,
            kw_in_psum, kw_ready, gates_exp_ready, gates_ready, v_aug_ready, v_mean_ready, gate_u_ready,
            neg_abs_ready, log_f_ready, low_ready, gate_z_ready, gate_den_ready, gate_rec_ready, gate_z2_ready,
            gate_q0_ready, gate_q1_ready, gate_q2_ready, gate_q3_ready, gate_q4_ready, rows_in_psum,
            heads_in_psum, rest_ready, run_max_ready, a_row_ready, sum_row_ready, parts_ready, exp_row_ready,
            max_log_ready, rest1_ready, part0_ready, rest2_ready, part1_ready, decay_log_in_psum, h_n_ready,
            decay_ready, h_ss_ready, h_sq_ready, norm_n_ready, floor_n_ready, norm_e_ready, norm_q_ready,
            h_var_ready, h_rstd_ready, h_s_ready, stage_a_done, scale_b_ready, clipped_ready, shifted_ready,
            magic_ready, expo_ready, x_q_ready, x_q_in_psum, stage_b_done, ffn_in_psum, x_q_t_ready, c_in_psum,
            stage_c_done, win_scores_in_psum, c_t_ready, att_t_ready, hid_in_psum, z_in_psum, hid_ready,
            pos_ready, tanh_z_ready, dist_ready, pos_gt_ready, pos_fl_ready, pos_r_ready, edge_ready,
            off_ready, edges_ready, off_sq_ready, outside_ready, scm_ready, dist2_ready, gauss_ready, pg_ready,
            kw_c_ready, prob_ready, neg_max_ready, den_ready, rden_ready, att_ready, att_in_psum, win_in_psum,
            x4_in_psum, y_ready, r_in_psum, x4_ready, k_in_psum, x_k_ready, k_act_ready, k_relu_ready,
            v_in_psum, r_tanh_ready, stage_d_done, stored,
        ) = [sem(name) for name in """
            q_in_psum weighted ctx_in_psum head_scores_done q_t_ready ctx_t_ready gates_in_psum
            kw_in_psum kw_ready gates_exp_ready gates_ready v_aug_ready v_mean_ready gate_u_ready
            neg_abs_ready log_f_ready low_ready gate_z_ready gate_den_ready gate_rec_ready gate_z2_ready
            gate_q0_ready gate_q1_ready gate_q2_ready gate_q3_ready gate_q4_ready rows_in_psum
            heads_in_psum rest_ready run_max_ready a_row_ready sum_row_ready parts_ready exp_row_ready
            max_log_ready rest1_ready part0_ready rest2_ready part1_ready decay_log_in_psum h_n_ready
            decay_ready h_ss_ready h_sq_ready norm_n_ready floor_n_ready norm_e_ready norm_q_ready
            h_var_ready h_rstd_ready h_s_ready stage_a_done scale_b_ready clipped_ready shifted_ready
            magic_ready expo_ready x_q_ready x_q_in_psum stage_b_done ffn_in_psum x_q_t_ready c_in_psum
            stage_c_done win_scores_in_psum c_t_ready att_t_ready hid_in_psum z_in_psum hid_ready
            pos_ready tanh_z_ready dist_ready pos_gt_ready pos_fl_ready pos_r_ready edge_ready
            off_ready edges_ready off_sq_ready outside_ready scm_ready dist2_ready gauss_ready pg_ready
            kw_c_ready prob_ready neg_max_ready den_ready rden_ready att_ready att_in_psum win_in_psum
            x4_in_psum y_ready r_in_psum x4_ready k_in_psum x_k_ready k_act_ready k_relu_ready
            v_in_psum r_tanh_ready stage_d_done stored
        """.split()]
        A_, B_, C_, D_ = range(4)

        bank_q = bank[0]
        bank_ctx = bank[1]
        gates_ps = bank[1][:, 0:48].rearrange("p (j c) -> p j c", j=TPG)
        rows_ps = bank[1][:, 128:128 + 2 * S].rearrange("p (k s) -> p k s", k=2)
        score_ps = [bank[k][:, :].rearrange("p (u j s) -> p u j s", u=2, j=TPG) for k in (0, 1)]
        decay_ps = [bank[k][:, :].rearrange("p (u j s) -> p u j s", u=2, j=TPG) for k in (2, 3)]
        heads_ps = banks[:, 2:4, 0:8 * (DH + 1)].rearrange("p k (c d) -> p k c d", d=DH + 1)
        exp_col_ps = bank[3][:, 480:496]
        ffn_ps = bank[4]
        xq_ps = bank[4][:, :].bitcast(BF16)[:, 0:GC]
        win_ps = bank[5][:, 0:TPG * S].rearrange("p (j s) -> p j s", j=TPG)
        z_ps = bank[5][:, TPG * S:TPG * S + TPG]
        att_ps = bank[6][:, 0:TPG * S].rearrange("p (j s) -> p j s", j=TPG)

        def flat3(view):
            return view.rearrange("p a b -> p (a b)")

        def flat4(view):
            return view.rearrange("p a b c -> p (a b c)")

        HALVES = (slice(0, S), slice(S, P))
        forget = flat3(gates[:, 1, :, :])
        input_exp, forget_exp = flat3(gates_exp[:, 0, :, :]), flat3(gates_exp[:, 1, :, :])
        iota_group = iota[:, :].unsqueeze(1).to_broadcast([P, TPG, S])
        iota_half_group = iota_half[:, :].unsqueeze(1).to_broadcast([P, TPG, S])
        window_ends = prob[:, :, 0:S:S - 1]
        sums = heads_ps[:, :, :, DH]
        floor_v = floor_n[:, :].rearrange("p (k c) -> p k c", k=2)
        norm_v = norm_n[:, :].rearrange("p (k c) -> p k c", k=2)

        def later(x):
            return x.rearrange("p (n s) -> p n s", s=S)[:, :, 1:S]

        def earlier(x):
            return x.rearrange("p (n s) -> p n s", s=S)[:, :, 0:S - 1]

        NSMALL = 10

        def started(g):
            return not (isinstance(g, int) and g <= 0)

        def first(g):
            return isinstance(g, int) and g == 0

        def steps(engine, step):
            for i in range(STEADY):
                step(i)
            with engine.Fori(STEADY, NG) as i:
                step(i)
            for i in range(NG, NG + LAST):
                step(i)

        def works(i, skew):
            return not isinstance(i, int) or 0 <= i - skew < NG

        block = stack.enter_context(nc.Block())

        @block.sync
        def _(sp):
            def load_weights():
                for n, w in ((WF, weight_fp8), (WA, W_a), (WP, W_p), (WR, W_r), (WK, W_k), (WV, W_v)):
                    rows = w.shape[0]
                    sp.dma_start(w_raw[0:rows, n, :], w).then_inc(w_loaded, 16)
                sp.dma_start(igk[:, :, :], igate_kernel.rearrange("(k c) h -> c k h", c=D)).then_inc(small_loaded, 16)
                sp.dma_start(fgk[:, :, :], fgate_kernel.rearrange("(k c) h -> c k h", c=D)).then_inc(small_loaded, 16)
                sp.dma_start(gate_bias[:, 0:NH], igate_bias.partition_broadcast(P)).then_inc(small_loaded, 16)
                sp.dma_start(gate_bias[:, NH:2 * NH], fgate_bias.partition_broadcast(P)).then_inc(small_loaded, 16)
                sp.dma_start(head_scale[:, :], outnorm_scale.partition_broadcast(P)).then_inc(small_loaded, 16)
                sp.dma_start(in_scale[:, :], input_scale.partition_broadcast(P)).then_inc(small_loaded, 16)
                sp.dma_start(w_scale[:, :], weight_scale.partition_broadcast(P)).then_inc(small_loaded, 16)
                sp.dma_start(mu[:, 0:1], mu_r.rearrange("(c a) -> c a", a=1)).then_inc(small_loaded, 16)
                sp.dma_start(mu[:, 1:2], mu_k.rearrange("(c a) -> c a", a=1)).then_inc(small_loaded, 16)
                sp.dma_start(vp_col[:, :], V_p.rearrange("a p -> p a")).then_inc(small_loaded, 16)
                sp.wait_ge(bias_cleared, 1)
                for p in (0, 64, 96):
                    sp.dma_start(bias_rows[p:p + 1, :], ffn_bias.rearrange("(a d) -> a d", a=1)).then_inc(bias_loaded, 16)

            def step(i):
                if works(i, 0):
                    g = i
                    if started(g):
                        sp.wait_ge(x_loaded, 16 * g)
                    sp.dma_start(x_all[:, g, :, :], x_dram[g]).then_inc(x_loaded, 16)
                if works(i, 5):
                    g = i - 5
                    if started(g):
                        sp.wait_ge(win_in_psum, g)
                    sp.dma_start(ctx_c[:, :, :], ctx_dram[g]).then_inc(ctx_c_loaded, 16)
                if works(i, 1):
                    g = i - 1
                    if started(g):
                        sp.wait_ge(ctx_in_psum, g)
                        sp.wait_ge(v_aug_ready, g)
                    sp.dma_start(ctx_a[:, :, :], ctx_dram[g]).then_inc(ctx_a_loaded, 16)
                    if first(g):
                        load_weights()
                if works(i, 7):
                    g = i - 7
                    sp.wait_ge(stage_d_done, g + 1)
                    sp.dma_start(out_dram[g], x_all[:, g, :, :]).then_inc(stored, 16)

            steps(sp, step)
            sp.wait_ge(stored, 16 * NG)

        @block.gpsimd
        def _(pool):
            pool.memset(bias_rows[:, :], 0.0).then_inc(bias_cleared, 1)
            pool.wait_ge(bias_cleared, 1)
            made = [0]

            def then(instruction):
                made[0] += 1
                instruction.then_inc(consts_step, 1)
                pool.wait_ge(consts_step, made[0])

            def cut(view, pattern, op, fill, base, cm=1):
                then(pool.affine_select(out=view, in_=view, pattern=pattern, compare_op=op, fill=fill,
                                        base=base, channel_multiplier=cm))

            then(pool.memset(half_power[:, :], -0.5))
            then(pool.memset(eps_col[:, :], EPS_NORM))
            then(pool.memset(ident[:, :], 1.0))
            cut(ident[:, :], [[-1, P]], ALU.is_equal, 0.0, 0)
            pool.tensor_copy(ident_bf[:, :], ident[:, :]).then_inc(ident_ready, 1)
            pool.wait_ge(ident_ready, 1)

            def make_constants():
                then(pool.memset(cum[:, :], 1.0))
                then(pool.memset(pick[:, :], 1.0))
                then(pool.memset(neg_cum[:, :], -1.0))
                then(pool.memset(batch_mask[:, :, :], 0.0))
                then(pool.memset(row_mask[:, :], 1.0))
                then(pool.memset(x_prev[:, :, 0:1], 0.0))
                then(pool.memset(v_aug[:, :, :, DH:DH + 1], 1.0))
                for b, half in enumerate(HALVES):
                    cut(cum[half, :], [[1, S]], ALU.is_ge, 0.0, 0, -1)
                    cut(neg_cum[half, :], [[1, S]], ALU.is_ge, 0.0, 0, -1)
                    cut(pick[half, :], [[1, S]], ALU.is_equal, 0.0, 0, -1)
                    then(pool.memset(batch_mask[half, :, b:b + 1], 1.0))
                for quad in range(4):
                    rows = slice(32 * quad, 32 * quad + 32)
                    cut(row_mask[rows, :], [[-16, 2]], ALU.is_ge, 0.0, 0)
                    cut(row_mask[rows, :], [[16, 2]], ALU.is_ge, 0.0, 15, -1)
                pool.memset(spare_pool[:, :], 0.0).then_inc(consts_ready, 1)
                then(pool.memset(ones_bf[:, :], 1.0))
                then(pool.memset(causal[:, :, :, :], 0.0))
                then(pool.memset(pick_of_row[:, :, :], 0.0))
                then(pool.memset(cols_of_row[:, :, :, :], 0.0))
                then(pool.memset(window_edge[:, :], -4.0 * BIG))
                then(pool.memset(back[:, :, :], 0.0))
                then(pool.iota(iota[:, :], [[1, S]], base=0, channel_multiplier=0,
                               allow_small_or_imprecise_dtypes=True))
                then(pool.tensor_scalar(iota_half[:, :], iota[:, :], 0.5, None, ALU.add))
                for quad in (0, 2, 3):
                    rows = slice(32 * quad, 32 * quad + 32)
                    cut(pick_of_row[rows, :, :], [[-1, 16], [-16, 2]], ALU.not_equal, 1.0, 0)
                    for b in range(2):
                        cut(cols_of_row[rows, :, :, :], [[-1, 2], [-2, 2], [-4, TPG]], ALU.not_equal, 1.0, -16 * b)
                pool.memset(spare_pool[:, :], 0.0).then_inc(consts_ready, 1)
                for b, half in enumerate(HALVES):
                    cut(causal[half, :, :, :].rearrange("p u j s -> p (u j) s"), [[0, 2 * TPG], [1, S]],
                        ALU.is_ge, -BIG, 0, -1)
                    cut(back[:, b, :], [[-1, 16]], ALU.not_equal, 1.0, -16 * b)
                pool.memset(spare_pool[:, :], 0.0).then_inc(consts_ready, 1)

            def step(i):
                if works(i, 5):
                    g = i - 5
                    pool.wait_ge(mean_ready[C_], TPG * g + TPG)
                    if started(g):
                        pool.wait_ge(rstd_ready[C_], g)
                    pool.tensor_tensor(var_eps[C_][:, :], mv[C_][:, :, 1], eps_col[:, 0:1].to_broadcast([P, TPG]), ALU.add)\
                        .then_inc(eps_added[C_], 1)
                    pool.wait_ge(eps_added[C_], g + 1)
                    if started(g):
                        pool.wait_ge(normed_ready[C_], TPG * g)
                    pool.tensor_tensor(rstd[C_][:, :], var_eps[C_][:, :], half_power[:, 0:TPG], ALU.pow).then_inc(rstd_ready[C_], 1)
                if works(i, 1):
                    g = i - 1
                    pool.wait_ge(mean_ready[A_], TPG * g + TPG)
                    if started(g):
                        pool.wait_ge(rstd_ready[A_], g)
                    pool.tensor_tensor(var_eps[A_][:, :], mv[A_][:, :, 1], eps_col[:, 0:1].to_broadcast([P, TPG]), ALU.add)\
                        .then_inc(eps_added[A_], 1)
                    pool.wait_ge(eps_added[A_], g + 1)
                    if started(g):
                        pool.wait_ge(normed_ready[A_], TPG * g)
                    pool.tensor_tensor(rstd[A_][:, :], var_eps[A_][:, :], half_power[:, 0:TPG], ALU.pow).then_inc(rstd_ready[A_], 1)
                    if first(g):
                        make_constants()
                if works(i, 4):
                    g = i - 4
                    pool.wait_ge(mean_ready[B_], TPG * g + TPG)
                    if started(g):
                        pool.wait_ge(rstd_ready[B_], g)
                    pool.tensor_tensor(var_eps[B_][:, :], mv[B_][:, :, 1], eps_col[:, 0:1].to_broadcast([P, TPG]), ALU.add)\
                        .then_inc(eps_added[B_], 1)
                    pool.wait_ge(eps_added[B_], g + 1)
                    if started(g):
                        pool.wait_ge(scale_b_ready, g)
                    pool.tensor_tensor(rstd[B_][:, :], var_eps[B_][:, :], half_power[:, 0:TPG], ALU.pow).then_inc(rstd_ready[B_], 1)
                    if first(g):
                        pool.wait_ge(weights_ready, 1)
                    pool.wait_ge(rstd_ready[B_], g + 1)
                    if started(g):
                        pool.wait_ge(normed_ready[B_], TPG * g)
                    pool.tensor_tensor(scale_b[:, :], rstd[B_][:, :], in_scale_inv[:, 0:1].to_broadcast([P, TPG]), ALU.mult)\
                        .then_inc(scale_b_ready, 1)
                if works(i, 6):
                    g = i - 6
                    pool.wait_ge(mean_ready[D_], TPG * g + TPG)
                    if started(g):
                        pool.wait_ge(rstd_ready[D_], g)
                    pool.tensor_tensor(var_eps[D_][:, :], mv[D_][:, :, 1], eps_col[:, 0:1].to_broadcast([P, TPG]), ALU.add)\
                        .then_inc(eps_added[D_], 1)
                    pool.wait_ge(eps_added[D_], g + 1)
                    if started(g):
                        pool.wait_ge(normed_ready[D_], TPG * g)
                    pool.tensor_tensor(rstd[D_][:, :], var_eps[D_][:, :], half_power[:, 0:TPG], ALU.pow).then_inc(rstd_ready[D_], 1)
                if works(i, 3):
                    g = i - 3
                    pool.wait_ge(h_var_ready, g + 1)
                    if started(g):
                        pool.wait_ge(h_n_ready, g)
                    pool.tensor_tensor(h_rstd[:, 0:8], h_var[:, 0:8], half_power[:, 0:8], ALU.pow).then_inc(h_rstd_ready, 1)
                    pool.wait_ge(h_var_ready, g + 1)
                    if started(g):
                        pool.wait_ge(h_n_ready, g)
                    pool.tensor_tensor(h_rstd[:, 8:16], h_var[:, 8:16], half_power[:, 8:16], ALU.pow).then_inc(h_rstd_ready, 1)
                if works(i, 7):
                    g = i - 7
                    pool.wait_ge(k_relu_ready, g + 1)
                    if started(g):
                        pool.wait_ge(v_in_psum, g)
                    pool.tensor_tensor(k_act[:, :], k_relu[:, :], k_relu[:, :], ALU.mult).then_inc(k_act_ready, 1)
                if works(i, 5):
                    g = i - 5
                    pool.wait_ge(pos_fl_ready, g + 1)
                    if started(g):
                        pool.wait_ge(off_sq_ready, g)
                    pool.tensor_tensor(off[:, :, :], iota_half_group, pos_fl[:, :].unsqueeze(2).to_broadcast([P, TPG, S]), ALU.subtract)\
                        .then_inc(off_ready, 1)
                    pool.wait_ge(pos_ready, g + 1)
                    if started(g):
                        pool.wait_ge(dist2_ready, g)
                    pool.tensor_tensor(dist[:, :, :], iota_group, pos[:, :].unsqueeze(2).to_broadcast([P, TPG, S]), ALU.subtract)\
                        .then_inc(dist_ready, 1)
                if works(i, 4):
                    g = i - 4
                    pool.wait_ge(magic_ready, g + 1)
                    if started(g):
                        pool.wait_ge(x_q_ready, g)
                    pool.tensor_tensor(shifted[:, :], clipped[:, :], magic[:, :], ALU.add).then_inc(shifted_ready, 1)
                if works(i, 2):
                    g = i - 2
                    pool.wait_ge(v_mean_ready, g + 1)
                    pool.wait_ge(ctx_a_loaded, 16 * (g + 1))
                    if started(g):
                        pool.wait_ge(heads_in_psum, 2 * g)
                    pool.tensor_tensor(v_aug[:, :, :, :].rearrange("p j h d -> p (j h) d")[:, :, 0:DH],
                                       ctx_a[:, :, :].rearrange("p j (h d) -> p (j h) d", h=NH),
                                       v_mean[:, :].unsqueeze(2).to_broadcast([P, 16, DH]), ALU.subtract).then_inc(v_aug_ready, 1)
                if works(i, 3):
                    g = i - 3
                    if first(g):
                        pool.wait_ge(small_loaded, 16 * NSMALL)
                    pool.wait_ge(h_n_ready, g + 1)
                    if started(g):
                        pool.wait_ge(stage_a_done, g)
                    pool.tensor_tensor(h_s[:, :, :], h_n[:, :, :].rearrange("p (j h) d -> p j (h d)", h=NH),
                                       head_scale[:, :].unsqueeze(1).to_broadcast([P, TPG, D]), ALU.mult).then_inc(h_s_ready, 1)
                if works(i, 5):
                    g = i - 5
                    pool.wait_ge(edges_ready, g + 1)
                    pool.wait_ge(gauss_ready, g + 1)
                    if started(g):
                        pool.wait_ge(att_ready, g)
                    pool.tensor_tensor(pg[:, :, :], prob[:, :, :], gauss[:, :, :], ALU.mult).then_inc(pg_ready, 1)
                if works(i, 7):
                    g = i - 7
                    pool.wait_ge(y_ready, g + 1)
                    pool.wait_ge(normed_ready[D_], TPG * g + TPG)
                    pool.tensor_tensor(x_all[:, g, :, :], x_all[:, g, :, :], y[:, :].rearrange("p (j d) -> p j d", j=TPG), ALU.add)\
                        .then_inc(stage_d_done, 1)
                if works(i, 3):
                    g = i - 3
                    pool.wait_ge(h_s_ready, g + 1)
                    pool.wait_ge(normed_ready[A_], TPG * g + TPG)
                    pool.tensor_tensor(x_all[:, g, :, :], x_all[:, g, :, :], h_s[:, :, :], ALU.add).then_inc(stage_a_done, 1)

            steps(pool, step)

        @block.scalar
        def _(act):
            def act_takes_wait(n):
                act.copy(spare_act[:, n:n + 1], ident[:, 0:1])

            def copy_weights():
                for n in (WA, WP, WK, WV):
                    act.wait_ge(w_transposed, n + 1)
                    rows = HID if n == WP else D
                    act.activation(w_t[:, n, 0:rows], bank[2 + n][:, 0:rows], ACT.Copy, scale=0.5 if n == WV else 1.0)                        .then_inc(w_copied, 1)

            def spread_constants():
                act.wait_ge(consts_ready, 2)
                act.copy(pick_row[:, :, :, :], pick_of_row[:, :, :].unsqueeze(3).to_broadcast([P, 16, 2, S]))                    .then_inc(consts_spread, 1)
                act.copy(row_cols[:, :, :, :, :].rearrange("p k u j s -> p (k u) j s"),
                         cols_of_row[:, :, :, :].rearrange("p k u j -> p (k u) j").unsqueeze(3)
                         .to_broadcast([P, 4, TPG, S])).then_inc(consts_spread, 1)

            act.wait_ge(ident_ready, 1)

            def step(i):
                if works(i, 7):
                    g = i - 7
                    act.wait_ge(x4_in_psum, g + 1)
                    if started(g):
                        act.wait_ge(k_in_psum, g)
                    act.activation(x_k[:, :], bank[7], ACT.Copy, scale=mu[:, 1:2]).then_inc(x4_ready, 1)
                if works(i, 6):
                    g = i - 6
                    act.wait_ge(att_in_psum, g + 1)
                    if started(g):
                        act.wait_ge(win_in_psum, g)
                    act.copy(att_t[:, :, :], att_ps).then_inc(att_t_ready, 1)
                if works(i, 2):
                    g = i - 2
                    act.wait_ge(ctx_in_psum, g + 1)
                    if started(g):
                        act.wait_ge(head_scores_done, NH * g)
                    act.copy(ctx_t[:, :], bank_ctx[:, :]).then_inc(ctx_t_ready, 1)
                    act.wait_ge(q_in_psum, g + 1)
                    if started(g):
                        act.wait_ge(head_scores_done, NH * g)
                    act.copy(q_t[:, :], bank_q[:, :]).then_inc(q_t_ready, 1)
                if works(i, 5):
                    g = i - 5
                    act.wait_ge(shift_ready[C_], g + 1)
                    if started(g):
                        act.wait_ge(c_in_psum, g)
                    act_takes_wait(C_)
                    for j in range(TPG):
                        act.activation(normed[C_][:, j, :], x_all[:, g, j, :], ACT.Identity, bias=shift[C_][:, j:j + 1],
                                       scale=rstd[C_][:, j:j + 1]).then_inc(normed_ready[C_], 1)
                if works(i, 3):
                    g = i - 3
                    act.wait_ge(heads_in_psum, 2 * g + 2)
                    if started(g):
                        act.wait_ge(h_ss_ready, g)
                    act.activation(h_sq[:, :, :].rearrange("p (k c) d -> p k c d", k=2), heads_ps[:, :, :, 0:DH], ACT.Square)\
                        .then_inc(h_sq_ready, 1)
                if works(i, 5):
                    g = i - 5
                    act.wait_ge(c_in_psum, g + 1)
                    if started(g):
                        act.wait_ge(win_scores_in_psum, g)
                    act.copy(c_t[:, :], bank[5][:, :]).then_inc(c_t_ready, 1)
                if works(i, 4):
                    g = i - 4
                    act.wait_ge(shift_ready[B_], g + 1)
                    if started(g):
                        act.wait_ge(clipped_ready, g)
                    act_takes_wait(B_)
                    for j in range(TPG):
                        act.activation(normed[B_][:, j, :], x_all[:, g, j, :], ACT.Identity, bias=shift[B_][:, j:j + 1],
                                       scale=scale_b[:, j:j + 1]).then_inc(normed_ready[B_], 1)
                if works(i, 2):
                    g = i - 2
                    act.wait_ge(neg_abs_ready, g + 1)
                    if started(g):
                        act.wait_ge(gate_z_ready, g)
                    act.activation(gate_u[:, :], neg_abs[:, :], ACT.Exp).then_inc(gate_u_ready, 1)
                    if first(g):
                        spread_constants()
                if works(i, 5):
                    g = i - 5
                    act.wait_ge(hid_in_psum, g + 1)
                    if started(g):
                        act.wait_ge(z_in_psum, g)
                    act.activation(hid[:, :], bank[6][0:HID, :], ACT.Tanh).then_inc(hid_ready, 1)
                if works(i, 7):
                    g = i - 7
                    act.wait_ge(k_in_psum, g + 1)
                    if started(g):
                        act.wait_ge(k_act_ready, g)
                    act.activation(k_relu[:, :], bank[7], ACT.Relu).then_inc(k_relu_ready, 1)
                if works(i, 5):
                    g = i - 5
                    act.wait_ge(z_in_psum, g + 1)
                    if started(g):
                        act.wait_ge(pos_ready, g)
                    act.activation(tanh_z[:, :], z_ps, ACT.Tanh, scale=0.5).then_inc(tanh_z_ready, 1)
                if works(i, 6):
                    g = i - 6
                    act.wait_ge(shift_ready[D_], g + 1)
                    if started(g):
                        act.wait_ge(x4_in_psum, g)
                    act_takes_wait(D_)
                    for j in range(TPG):
                        act.activation(normed[D_][:, j, :], x_all[:, g, j, :], ACT.Identity, bias=shift[D_][:, j:j + 1],
                                       scale=rstd[D_][:, j:j + 1]).then_inc(normed_ready[D_], 1)
                if works(i, 7):
                    g = i - 7
                    act.wait_ge(r_in_psum, g + 1)
                    if started(g):
                        act.wait_ge(y_ready, g)
                    act.activation(r_tanh[:, :], bank[7], ACT.Tanh, scale=0.5).then_inc(r_tanh_ready, 1)
                if works(i, 2):
                    g = i - 2
                    act.wait_ge(kw_in_psum, g + 1)
                    act_takes_wait(4)
                    act.copy(kw_all[:, g, :], bank_q[:, :]).then_inc(kw_ready, 1)
                if works(i, 5):
                    g = i - 5
                    act.wait_ge(off_ready, g + 1)
                    if started(g):
                        act.wait_ge(outside_ready, g)
                    act.activation(off_sq[:, :, :], off[:, :, :], ACT.Square).then_inc(off_sq_ready, 1)
                    act.wait_ge(off_sq_ready, g + 1)
                    if started(g):
                        act.wait_ge(scm_ready, g)
                    act.activation(outside[:, :, :], off_sq[:, :, :], ACT.Relu, bias=window_edge[:, 0:1], scale=BIG).then_inc(outside_ready, 1)
                    act.wait_ge(dist_ready, g + 1)
                    if started(g):
                        act.wait_ge(gauss_ready, g)
                    act.activation(dist2[:, :, :], dist[:, :, :], ACT.Square).then_inc(dist2_ready, 1)
                if works(i, 4):
                    g = i - 4
                    act.wait_ge(kw_ready, g + 1)
                    if started(g):
                        act.wait_ge(win_scores_in_psum, g)
                    act_takes_wait(5)
                    act.copy(kw_c[:, :], kw_all[:, g, :]).then_inc(kw_c_ready, 1)
                if works(i, 5):
                    g = i - 5
                    act.wait_ge(dist2_ready, g + 1)
                    if started(g):
                        act.wait_ge(pg_ready, g)
                    act.activation(gauss[:, :, :], dist2[:, :, :], ACT.Exp, scale=-0.5).then_inc(gauss_ready, 1)
                    act.wait_ge(neg_max_ready, g + 1)
                    if started(g):
                        act.wait_ge(pg_ready, g)
                        act.wait_ge(den_ready, g)
                    for j in range(TPG):
                        act.activation(prob[:, j, :], scm[:, j, :], ACT.Exp, bias=neg_max[:, j:j + 1]).then_inc(prob_ready, 1)
                if works(i, 2):
                    g = i - 2
                    act.wait_ge(max_log_ready, g + 1)
                    if started(g):
                        act.wait_ge(heads_in_psum, 2 * g)
                    act.activation(exp_row[:, :], max_log[:, :], ACT.Exp, scale=-1.0).then_inc(exp_row_ready, 1)
                if works(i, 4):
                    g = i - 4
                    act.wait_ge(x_q_in_psum, g + 1)
                    if started(g):
                        act.wait_ge(ffn_in_psum, g)
                    act.copy(x_q_t[:, :], xq_ps).then_inc(x_q_t_ready, 1)
                if works(i, 2):
                    g = i - 2
                    act.wait_ge(decay_log_in_psum, 2 * g + 1)
                    if started(g):
                        act.wait_ge(weighted, 2 * g - 1)
                    act.activation(decay[:, 0, :, :, :], decay_ps[0], ACT.Exp).then_inc(decay_ready, 1)
                    act.wait_ge(decay_log_in_psum, 2 * g + 2)
                    if started(g):
                        act.wait_ge(weighted, 2 * g)
                    act.activation(decay[:, 1, :, :, :], decay_ps[1], ACT.Exp).then_inc(decay_ready, 1)
                if works(i, 1):
                    g = i - 1
                    act.wait_ge(shift_ready[A_], g + 1)
                    if started(g):
                        act.wait_ge(q_in_psum, g)
                    act_takes_wait(A_)
                    for j in range(TPG):
                        act.activation(normed[A_][:, j, :], x_all[:, g, j, :], ACT.Identity, bias=shift[A_][:, j:j + 1],
                                       scale=rstd[A_][:, j:j + 1]).then_inc(normed_ready[A_], 1)
                    if first(g):
                        copy_weights()
                if works(i, 6):
                    g = i - 6
                    act.wait_ge(x4_in_psum, g + 1)
                    if started(g):
                        act.wait_ge(r_in_psum, g)
                    act.copy(x_now[:, :], bank[7]).then_inc(x4_ready, 1)
                    act.wait_ge(x4_in_psum, g + 1)
                    if started(g):
                        act.wait_ge(r_in_psum, g)
                    act.copy(x_prev[:, :, 1:S], bank[7].rearrange("p (n s) -> p n s", s=S)[:, :, 0:S - 1]).then_inc(x4_ready, 1)

            steps(act, step)

        @block.vector
        def _(dve):
            done = [0]

            def then(instruction):
                done[0] += 1
                instruction.then_inc(split_step, 1)
                dve.wait_ge(split_step, done[0])

            def prepare_gate_weights():
                for c in (gate_w_q, gate_w_c):
                    then(dve.memset(c[:, :], 0.0))
                dve.wait_ge(small_loaded, 16 * NSMALL)
                for h in range(NH):
                    then(dve.memset(gate_w_c[DH * h:DH * h + DH, 2 * NH + h:2 * NH + h + 1], 1.0 / DH))
                for n, w in ((0, igk), (NH, fgk)):
                    then(dve.tensor_copy(gate_w_q[:, n:n + NH], w[:, 0, :]))
                    then(dve.tensor_tensor(gate_w_c[:, n:n + NH], w[:, 1, :], w[:, 2, :], ALU.add))
                then(dve.reciprocal(in_scale_inv[:, :], in_scale[:, :]))
                dve.tensor_scalar(one_less_mu[:, :], mu[:, :], -1.0, 1.0, ALU.mult, ALU.add)                    .then_inc(gate_weights_ready, 1)

            def prepare_weights():
                dve.wait_ge(w_transposed, NW)
                for n, share in enumerate((mu, one_less_mu)):
                    then(dve.tensor_scalar(w_mix[:, n, :], bank[2 + WR][:, 0:D], share[:, 0:1], None, ALU.mult))
                then(dve.tensor_scalar(w_rest[:, 0, :], bank[2 + WF][:, 0:D], w_scale[:, 0:1], in_scale[:, 0:1],
                                       ALU.mult, ALU.mult))
                then(dve.tensor_copy(w_parts[:, 0, :], w_rest[:, 0, :]))
                then(dve.tensor_tensor(w_rest[:, 1, :], w_rest[:, 0, :], w_parts[:, 0, :], ALU.subtract))
                then(dve.tensor_copy(w_parts[:, 1, :], w_rest[:, 1, :]))
                then(dve.tensor_tensor(w_rest[:, 0, :], w_rest[:, 1, :], w_parts[:, 1, :], ALU.subtract))
                then(dve.tensor_copy(w_parts[:, 2, :], w_rest[:, 0, :]))
                dve.wait_ge(bias_loaded, 16 * 3)
                then(dve.tensor_copy(bias_tmp[64:128, 0, :], bias_rows[64:128, :]))
                then(dve.tensor_tensor(bias_rows[64:128, :], bias_rows[64:128, :], bias_tmp[64:128, 0, :], ALU.subtract))
                then(dve.tensor_copy(bias_tmp[96:128, 1, :], bias_rows[96:128, :]))
                then(dve.tensor_tensor(bias_rows[96:128, :], bias_rows[96:128, :], bias_tmp[96:128, 1, :], ALU.subtract))
                dve.tensor_copy(bias_parts[:, :, :], bias_rows[:, :].unsqueeze(1).to_broadcast([P, TPG, D]))\
                    .then_inc(weights_ready, 1)

            def dve_takes_wait(n):
                dve.memset(spare[:, n:n + 1], 0.0)

            def step(i):
                if works(i, 5):
                    g = i - 5
                    dve.wait_ge(ffn_in_psum, g + 1)
                    dve.tensor_tensor(x_all[:, g, :, :], ffn_ps.rearrange("p (j d) -> p j d", j=TPG), x_all[:, g, :, :], ALU.add)\
                        .then_inc(stage_b_done, 1)
                    dve.wait_ge(stage_b_done, g + 1)
                    if started(g):
                        dve.wait_ge(mean_ready[C_], TPG * g)
                    dve_takes_wait(C_)
                    for j in range(TPG):
                        dve.bn_stats(stats[C_][:, j, :], x_all[:, g, j, :]).then_inc(stats_done[C_], 1)
                    dve.wait_ge(stats_done[C_], TPG * g + TPG)
                    if started(g):
                        dve.wait_ge(shift_ready[C_], g)
                    dve_takes_wait(C_)
                    for j in range(TPG):
                        dve.bn_aggr(mv[C_][:, j, :], stats[C_][:, j, :]).then_inc(mean_ready[C_], 1)
                if works(i, 7):
                    g = i - 7
                    dve.wait_ge(x4_ready, 3 * g + 3)
                    dve.scalar_tensor_tensor(out=later(x_k[:, :]), in0=earlier(bank[7]), scalar=one_less_mu[:, 1:2], in1=later(x_k[:, :]),
                                             op0=ALU.mult, op1=ALU.add).then_inc(x_k_ready, 1)
                if works(i, 4):
                    g = i - 4
                    dve.wait_ge(stage_a_done, g + 1)
                    if started(g):
                        dve.wait_ge(mean_ready[B_], TPG * g)
                    dve_takes_wait(B_)
                    for j in range(TPG):
                        dve.bn_stats(stats[B_][:, j, :], x_all[:, g, j, :]).then_inc(stats_done[B_], 1)
                if works(i, 5):
                    g = i - 5
                    dve.wait_ge(rstd_ready[C_], g + 1)
                    if started(g):
                        dve.wait_ge(normed_ready[C_], TPG * g)
                    dve.scalar_tensor_tensor(out=shift[C_][:, :], in0=mv[C_][:, :, 0], scalar=-1.0, in1=rstd[C_][:, :], op0=ALU.mult,
                                             op1=ALU.mult).then_inc(shift_ready[C_], 1)
                if works(i, 4):
                    g = i - 4
                    dve.wait_ge(stats_done[B_], TPG * g + TPG)
                    if started(g):
                        dve.wait_ge(shift_ready[B_], g)
                    dve_takes_wait(B_)
                    for j in range(TPG):
                        dve.bn_aggr(mv[B_][:, j, :], stats[B_][:, j, :]).then_inc(mean_ready[B_], 1)
                if works(i, 6):
                    g = i - 6
                    dve.wait_ge(win_in_psum, g + 1)
                    dve.tensor_tensor(x_all[:, g, :, :], bank[5].rearrange("p (j d) -> p j d", j=TPG), x_all[:, g, :, :], ALU.add)\
                        .then_inc(stage_c_done, 1)
                if works(i, 0):
                    g = i
                    dve.wait_ge(x_loaded, 16 * (g + 1))
                    if started(g):
                        dve.wait_ge(mean_ready[A_], TPG * g)
                    dve_takes_wait(A_)
                    for j in range(TPG):
                        dve.bn_stats(stats[A_][:, j, :], x_all[:, g, j, :]).then_inc(stats_done[A_], 1)
                if works(i, 6):
                    g = i - 6
                    dve.wait_ge(stage_c_done, g + 1)
                    if started(g):
                        dve.wait_ge(mean_ready[D_], TPG * g)
                    dve_takes_wait(D_)
                    for j in range(TPG):
                        dve.bn_stats(stats[D_][:, j, :], x_all[:, g, j, :]).then_inc(stats_done[D_], 1)
                if works(i, 4):
                    g = i - 4
                    dve.wait_ge(scale_b_ready, g + 1)
                    if started(g):
                        dve.wait_ge(normed_ready[B_], TPG * g)
                    dve.scalar_tensor_tensor(out=shift[B_][:, :], in0=mv[B_][:, :, 0], scalar=-1.0, in1=scale_b[:, :], op0=ALU.mult,
                                             op1=ALU.mult).then_inc(shift_ready[B_], 1)
                if works(i, 6):
                    g = i - 6
                    dve.wait_ge(stats_done[D_], TPG * g + TPG)
                    if started(g):
                        dve.wait_ge(shift_ready[D_], g)
                    dve_takes_wait(D_)
                    for j in range(TPG):
                        dve.bn_aggr(mv[D_][:, j, :], stats[D_][:, j, :]).then_inc(mean_ready[D_], 1)
                if works(i, 3):
                    g = i - 3
                    dve.wait_ge(h_sq_ready, g + 1)
                    if started(g):
                        dve.wait_ge(norm_n_ready, g)
                    dve.tensor_copy(floor_n[:, :], exp_col_ps).then_inc(floor_n_ready, 1)
                    dve.wait_ge(floor_n_ready, 2 * g + 1)
                    dve.scalar_tensor_tensor(out=floor_v, in0=sums, scalar=-1.0, in1=floor_v, op0=ALU.mult, op1=ALU.max)\
                        .then_inc(floor_n_ready, 1)
                    dve.wait_ge(floor_n_ready, 2 * g + 2)
                    if started(g):
                        dve.wait_ge(norm_e_ready, g)
                    dve.tensor_tensor(norm_v, sums, floor_v, ALU.max).then_inc(norm_n_ready, 1)
                    dve.wait_ge(h_sq_ready, g + 1)
                    if started(g):
                        dve.wait_ge(h_var_ready, g)
                    dve.tensor_reduce(h_ss[:, :], h_sq[:, :, :], AX_X, ALU.add).then_inc(h_ss_ready, 1)
                    dve.wait_ge(norm_n_ready, g + 1)
                    if started(g):
                        dve.wait_ge(norm_q_ready, g)
                    dve.tensor_scalar(norm_e[:, :], norm_n[:, :], EPS_BACKEND, None, ALU.add).then_inc(norm_e_ready, 1)
                if works(i, 2):
                    g = i - 2
                    dve.wait_ge(gates_in_psum, 2 * g + 2)
                    if started(g):
                        dve.wait_ge(gates_exp_ready, g)
                    for k in range(2):
                        dve.tensor_tensor(gates[:, k, :, :], gates_ps[:, :, NH * k:NH * k + NH],
                                          gate_bias[:, NH * k:NH * k + NH].unsqueeze(1).to_broadcast([P, TPG, NH]), ALU.add)\
                            .then_inc(gates_ready, 1)
                if works(i, 3):
                    g = i - 3
                    dve.wait_ge(norm_e_ready, g + 1)
                    if started(g):
                        dve.wait_ge(h_var_ready, g)
                    dve.scalar_tensor_tensor(out=norm_q[:, :], in0=norm_e[:, :], scalar=EPS_HEAD, in1=norm_e[:, :], op0=ALU.mult,
                                             op1=ALU.mult).then_inc(norm_q_ready, 1)
                if works(i, 2):
                    g = i - 2
                    dve.wait_ge(gates_ready, 2 * g + 2)
                    if started(g):
                        dve.wait_ge(gate_u_ready, g)
                    dve.scalar_tensor_tensor(out=neg_abs[:, :], in0=forget, scalar=-1.0, in1=forget, op0=ALU.mult, op1=ALU.min)\
                        .then_inc(neg_abs_ready, 1)
                if works(i, 3):
                    g = i - 3
                    dve.wait_ge(h_ss_ready, g + 1)
                    dve.wait_ge(norm_q_ready, g + 1)
                    if started(g):
                        dve.wait_ge(h_rstd_ready, 2 * g)
                    dve.scalar_tensor_tensor(out=h_var[:, :], in0=h_ss[:, :], scalar=1.0 / DH, in1=norm_q[:, :], op0=ALU.mult,
                                             op1=ALU.add).then_inc(h_var_ready, 1)
                if works(i, 4):
                    g = i - 4
                    dve.wait_ge(normed_ready[B_], TPG * g + TPG)
                    if started(g):
                        dve.wait_ge(shifted_ready, g)
                    dve.tensor_scalar(clipped[:, :], normed[B_][:, :, :].rearrange("p j d -> p (j d)"), FP8_MAX, -FP8_MAX, ALU.min,
                                      ALU.max).then_inc(clipped_ready, 1)
                if works(i, 2):
                    g = i - 2
                    dve.wait_ge(gate_u_ready, g + 1)
                    dve.tensor_scalar(gate_den[:, :], gate_u[:, :], 2.0, None, ALU.add).then_inc(gate_den_ready, 1)
                    dve.wait_ge(gates_in_psum, 2 * g + 2)
                    if started(g):
                        dve.wait_ge(v_aug_ready, g)
                    dve.tensor_copy(v_mean[:, :].rearrange("p (j h) -> p j h", h=NH), gates_ps[:, :, 2 * NH:3 * NH])\
                        .then_inc(v_mean_ready, 1)
                    dve.wait_ge(gate_den_ready, g + 1)
                    dve.reciprocal(gate_rec[:, :], gate_den[:, :]).then_inc(gate_rec_ready, 1)
                if works(i, 6):
                    g = i - 6
                    dve.wait_ge(rstd_ready[D_], g + 1)
                    if started(g):
                        dve.wait_ge(normed_ready[D_], TPG * g)
                    dve.scalar_tensor_tensor(out=shift[D_][:, :], in0=mv[D_][:, :, 0], scalar=-1.0, in1=rstd[D_][:, :], op0=ALU.mult,
                                             op1=ALU.mult).then_inc(shift_ready[D_], 1)
                if works(i, 2):
                    g = i - 2
                    dve.wait_ge(gate_rec_ready, g + 1)
                    dve.tensor_tensor(gate_z[:, :], gate_u[:, :], gate_rec[:, :], ALU.mult).then_inc(gate_z_ready, 1)
                    dve.wait_ge(gate_z_ready, g + 1)
                    dve.tensor_tensor(gate_z2[:, :], gate_z[:, :], gate_z[:, :], ALU.mult).then_inc(gate_z2_ready, 1)
                    dve.wait_ge(gate_z2_ready, g + 1)
                    dve.tensor_scalar(gate_q[0][:, :], gate_z2[:, :], ATANH[4], None, ALU.mult).then_inc(gate_q0_ready, 1)
                    dve.wait_ge(gate_q0_ready, g + 1)
                    dve.scalar_tensor_tensor(out=gate_q[1][:, :], in0=gate_q[0][:, :], scalar=ATANH[3], in1=gate_z2[:, :], op0=ALU.add,
                                             op1=ALU.mult).then_inc(gate_q1_ready, 1)
                if works(i, 4):
                    g = i - 4
                    dve.wait_ge(clipped_ready, g + 1)
                    if started(g):
                        dve.wait_ge(magic_ready, g)
                    dve.tensor_scalar(expo[:, :].bitcast(U32), clipped[:, :].bitcast(U32), 0x7F800000, None, ALU.bitwise_and)\
                        .then_inc(expo_ready, 1)
                if works(i, 2):
                    g = i - 2
                    dve.wait_ge(gate_q1_ready, g + 1)
                    dve.scalar_tensor_tensor(out=gate_q[2][:, :], in0=gate_q[1][:, :], scalar=ATANH[2], in1=gate_z2[:, :], op0=ALU.add,
                                             op1=ALU.mult).then_inc(gate_q2_ready, 1)
                    dve.wait_ge(gates_ready, 2 * g + 2)
                    if started(g):
                        dve.wait_ge(log_f_ready, g)
                    dve.tensor_scalar(low[:, :], forget, 0.0, None, ALU.min).then_inc(low_ready, 1)
                    dve.wait_ge(gate_q2_ready, g + 1)
                    dve.scalar_tensor_tensor(out=gate_q[3][:, :], in0=gate_q[2][:, :], scalar=ATANH[1], in1=gate_z2[:, :], op0=ALU.add,
                                             op1=ALU.mult).then_inc(gate_q3_ready, 1)
                if works(i, 5):
                    g = i - 5
                    dve.wait_ge(tanh_z_ready, g + 1)
                    if started(g):
                        dve.wait_ge(dist_ready, g)
                        dve.wait_ge(pos_gt_ready, g)
                    dve.tensor_scalar(pos[:, :], tanh_z[:, :], S / 2.0, S / 2.0, ALU.mult, ALU.add).then_inc(pos_ready, 1)
                if works(i, 2):
                    g = i - 2
                    dve.wait_ge(gate_q3_ready, g + 1)
                    dve.scalar_tensor_tensor(out=gate_q[4][:, :], in0=gate_q[3][:, :], scalar=ATANH[0], in1=gate_z[:, :], op0=ALU.add,
                                             op1=ALU.mult).then_inc(gate_q4_ready, 1)
                if works(i, 5):
                    g = i - 5
                    dve.wait_ge(pos_ready, g + 1)
                    if started(g):
                        dve.wait_ge(pos_fl_ready, g)
                    dve.tensor_scalar(pos_r[:, :], pos[:, :], ROUND_INT, -ROUND_INT, ALU.add, ALU.add).then_inc(pos_r_ready, 1)
                if works(i, 2):
                    g = i - 2
                    dve.wait_ge(gate_q4_ready, g + 1)
                    dve.wait_ge(low_ready, g + 1)
                    dve.scalar_tensor_tensor(out=forget, in0=gate_q[4][:, :], scalar=-2.0, in1=low[:, :], op0=ALU.mult, op1=ALU.add)\
                        .then_inc(log_f_ready, 1)
                if works(i, 5):
                    g = i - 5
                    dve.wait_ge(pos_r_ready, g + 1)
                    dve.tensor_tensor(pos_gt[:, :], pos_r[:, :], pos[:, :], ALU.is_gt).then_inc(pos_gt_ready, 1)
                if works(i, 2):
                    g = i - 2
                    if first(g):
                        dve.wait_ge(consts_ready, 1)
                    dve.wait_ge(log_f_ready, g + 1)
                    if started(g):
                        dve.wait_ge(rows_in_psum, g)
                    dve.tensor_tensor(gates_exp[:, :, :, :],
                                      gates[:, :, :, :].rearrange("p k j h -> p k (j h)").unsqueeze(2).to_broadcast([P, 2, 8, 16]),
                                      batch_mask[:, :, :].rearrange("p r b -> p (r b)").unsqueeze(1).unsqueeze(3)
                                      .to_broadcast([P, 2, 8, 16]), ALU.mult).then_inc(gates_exp_ready, 1)
                    if first(g):
                        prepare_weights()
                if works(i, 4):
                    g = i - 4
                    dve.wait_ge(expo_ready, g + 1)
                    if started(g):
                        dve.wait_ge(x_q_ready, g)
                    dve.tensor_scalar(magic[:, :], expo[:, :], E4M3_MIN_NORMAL, ROUND_E4M3, ALU.max, ALU.mult).then_inc(magic_ready, 1)
                if works(i, 3):
                    g = i - 3
                    dve.wait_ge(h_rstd_ready, 2 * g + 2)
                    if started(g):
                        dve.wait_ge(h_s_ready, g)
                    dve.tensor_tensor(h_n[:, :, :].rearrange("p (k c) d -> p k c d", k=2), heads_ps[:, :, :, 0:DH],
                                      h_rstd[:, :].rearrange("p (k c) -> p k c", k=2).unsqueeze(3).to_broadcast([P, 2, 8, DH]),
                                      ALU.mult).then_inc(h_n_ready, 1)
                if works(i, 2):
                    g = i - 2
                    dve.wait_ge(rows_in_psum, g + 1)
                    if started(g):
                        dve.wait_ge(rest_ready, 2 * g)
                        dve.wait_ge(run_max_ready, g)
                    dve.tensor_copy(a_row[:, :], rows_ps[:, 1, :]).then_inc(a_row_ready, 1)
                if works(i, 5):
                    g = i - 5
                    dve.wait_ge(pos_gt_ready, g + 1)
                    if started(g):
                        dve.wait_ge(edge_ready, 2 * g)
                        dve.wait_ge(off_ready, g)
                    dve.tensor_tensor(pos_fl[:, :], pos_r[:, :], pos_gt[:, :], ALU.subtract).then_inc(pos_fl_ready, 1)
                if works(i, 2):
                    g = i - 2
                    dve.wait_ge(a_row_ready, g + 1)
                    if started(g):
                        dve.wait_ge(rest_ready, 2 * g)
                        dve.wait_ge(sum_row_ready, g)
                    dve.tensor_tensor_scan(run_max[:, :], a_row[:, :], a_row[:, :], -3.0e38, ALU.max, ALU.max).then_inc(run_max_ready, 1)
                    dve.wait_ge(a_row_ready, g + 1)
                    if started(g):
                        dve.wait_ge(parts_ready, g)
                    dve.tensor_tensor(rest[:, 0:2, :], a_row[:, :].unsqueeze(1).to_broadcast([P, 2, S]),
                                      row_mask[:, :].unsqueeze(2).to_broadcast([P, 2, S]), ALU.mult).then_inc(rest_ready, 1)
                    dve.wait_ge(run_max_ready, g + 1)
                    if started(g):
                        dve.wait_ge(parts_ready, g)
                    dve.tensor_scalar(rest[:, 2, :], run_max[:, :], -1.0, None, ALU.mult).then_inc(rest_ready, 1)
                if works(i, 1):
                    g = i - 1
                    dve.wait_ge(rstd_ready[A_], g + 1)
                    if started(g):
                        dve.wait_ge(normed_ready[A_], TPG * g)
                    dve.scalar_tensor_tensor(out=shift[A_][:, :], in0=mv[A_][:, :, 0], scalar=-1.0, in1=rstd[A_][:, :], op0=ALU.mult,
                                             op1=ALU.mult).then_inc(shift_ready[A_], 1)
                    if first(g):
                        prepare_gate_weights()
                if works(i, 2):
                    g = i - 2
                    dve.wait_ge(rest_ready, 2 * g + 2)
                    if started(g):
                        dve.wait_ge(rest1_ready, g)
                    dve.tensor_copy(part_tmp[64:128, 0, :, :], rest[64:128, :, :]).then_inc(part0_ready, 1)
                    dve.wait_ge(run_max_ready, g + 1)
                    if started(g):
                        dve.wait_ge(exp_row_ready, g)
                    dve.tensor_tensor(max_log[:, :], rows_ps[:, 0, :], run_max[:, :], ALU.add).then_inc(sum_row_ready, 1)
                    dve.wait_ge(part0_ready, g + 1)
                    dve.tensor_tensor(rest[64:128, :, :], rest[64:128, :, :], part_tmp[64:128, 0, :, :], ALU.subtract)\
                        .then_inc(rest1_ready, 1)
                    dve.wait_ge(rest1_ready, g + 1)
                    if started(g):
                        dve.wait_ge(rest2_ready, g)
                    dve.tensor_copy(part_tmp[96:128, 1, :, :], rest[96:128, :, :]).then_inc(part1_ready, 1)
                    dve.wait_ge(part1_ready, g + 1)
                    dve.tensor_tensor(rest[96:128, :, :], rest[96:128, :, :], part_tmp[96:128, 1, :, :], ALU.subtract)\
                        .then_inc(rest2_ready, 1)
                    dve.wait_ge(rest2_ready, g + 1)
                    if started(g):
                        dve.wait_ge(decay_log_in_psum, 2 * g)
                    dve.tensor_copy(parts[:, :, :], rest[:, :, :]).then_inc(parts_ready, 1)
                if works(i, 5):
                    g = i - 5
                    dve.wait_ge(win_scores_in_psum, g + 1)
                    dve.wait_ge(outside_ready, g + 1)
                    if started(g):
                        dve.wait_ge(prob_ready, TPG * g)
                    dve.tensor_tensor(scm[:, :, :], win_ps, outside[:, :, :], ALU.subtract).then_inc(scm_ready, 1)
                    dve.wait_ge(scm_ready, g + 1)
                    if started(g):
                        dve.wait_ge(prob_ready, TPG * g)
                    dve.tensor_reduce(neg_max[:, :], scm[:, :, :], AX_X, ALU.max, negate=True).then_inc(neg_max_ready, 1)
                if works(i, 4):
                    g = i - 4
                    dve.wait_ge(shifted_ready, g + 1)
                    if started(g):
                        dve.wait_ge(x_q_in_psum, g)
                    dve.tensor_tensor(x_q[:, :, :].rearrange("p j d -> p (j d)"), shifted[:, :], magic[:, :], ALU.subtract)\
                        .then_inc(x_q_ready, 1)
                if works(i, 5):
                    g = i - 5
                    dve.wait_ge(pos_fl_ready, g + 1)
                    if started(g):
                        dve.wait_ge(edges_ready, g)
                    dve.tensor_scalar(edge[:, :, 0], pos_fl[:, :], -1.0, 3.0, ALU.mult, ALU.add).then_inc(edge_ready, 1)
                    dve.tensor_scalar(edge[:, :, 1], pos_fl[:, :], 3.0 - S, None, ALU.add).then_inc(edge_ready, 1)
                if works(i, 2):
                    g = i - 2
                    dve.wait_ge(sum_row_ready, g + 1)
                    dve.tensor_scalar(max_log[:, :], max_log[:, :], MIN_LOG, None, ALU.max).then_inc(max_log_ready, 1)
                if works(i, 7):
                    g = i - 7
                    dve.wait_ge(v_in_psum, g + 1)
                    dve.wait_ge(r_tanh_ready, g + 1)
                    if started(g):
                        dve.wait_ge(stage_d_done, g)
                    dve.scalar_tensor_tensor(out=y[:, :], in0=r_tanh[:, :], scalar=1.0, in1=bank[7], op0=ALU.add, op1=ALU.mult)\
                        .then_inc(y_ready, 1)
                if works(i, 5):
                    g = i - 5
                    dve.wait_ge(prob_ready, TPG * g + TPG)
                    dve.wait_ge(edge_ready, 2 * g + 2)
                    dve.scalar_tensor_tensor(out=window_ends, in0=edge[:, :, :], scalar=1.0, in1=window_ends, op0=ALU.max, op1=ALU.mult)\
                        .then_inc(edges_ready, 1)
                    dve.wait_ge(edges_ready, g + 1)
                    if started(g):
                        dve.wait_ge(rden_ready, g)
                    dve.tensor_reduce(den[:, :], prob[:, :, :], AX_X, ALU.add).then_inc(den_ready, 1)
                if works(i, 0):
                    g = i
                    dve.wait_ge(stats_done[A_], TPG * g + TPG)
                    if started(g):
                        dve.wait_ge(shift_ready[A_], g)
                    dve_takes_wait(A_)
                    for j in range(TPG):
                        dve.bn_aggr(mv[A_][:, j, :], stats[A_][:, j, :]).then_inc(mean_ready[A_], 1)
                if works(i, 5):
                    g = i - 5
                    dve.wait_ge(den_ready, g + 1)
                    if started(g):
                        dve.wait_ge(att_ready, g)
                    dve.reciprocal(rden[:, :], den[:, :]).then_inc(rden_ready, 1)
                if works(i, 2):
                    g = i - 2
                    dve.wait_ge(head_scores_done, NH * g + NH - 1)
                    dve.wait_ge(decay_ready, 2 * g + 1)
                    if started(g):
                        dve.wait_ge(heads_in_psum, 2 * g)
                    dve.scalar_tensor_tensor(out=flat4(weights[:, 0, :, :, :]), in0=bank[0], scalar=float(DH) ** -0.5,
                                             in1=flat4(decay[:, 0, :, :, :]), op0=ALU.mult, op1=ALU.mult).then_inc(weighted, 1)
                if works(i, 5):
                    g = i - 5
                    dve.wait_ge(pg_ready, g + 1)
                    dve.wait_ge(rden_ready, g + 1)
                    if started(g):
                        dve.wait_ge(att_in_psum, g)
                    dve.tensor_tensor(att[:, :, :], pg[:, :, :], rden[:, :].unsqueeze(2).to_broadcast([P, TPG, S]), ALU.mult)\
                        .then_inc(att_ready, 1)
                if works(i, 2):
                    g = i - 2
                    dve.wait_ge(head_scores_done, NH * g + NH)
                    dve.wait_ge(decay_ready, 2 * g + 2)
                    if started(g):
                        dve.wait_ge(heads_in_psum, 2 * g)
                    dve.scalar_tensor_tensor(out=flat4(weights[:, 1, :, :, :]), in0=bank[1], scalar=float(DH) ** -0.5,
                                             in1=flat4(decay[:, 1, :, :, :]), op0=ALU.mult, op1=ALU.mult).then_inc(weighted, 1)

            steps(dve, step)

        @block.tensor
        def _(pe):
            def pe_takes_wait():
                pe.matmul(bank[6][0:32, 508:510], ident_bf[:, 0:32], ident_bf[:, 0:2], start=True, stop=True)

            def transpose_weights():
                pe.wait_ge(w_loaded, 16 * NW)
                for n in range(NW):
                    rows = HID if n == WP else D
                    pe.transpose(bank[2 + n][:, 0:rows], w_raw[0:rows, n, :], ident[0:rows, 0:rows])\
                        .then_inc(w_transposed, 1)

            def decay_product(k):
                pe.matmul(bank[2 + k], ident_bf[:, :], causal[:, :, :, :], start=True, stop=False)
                pe.matmul(bank[2 + k], parts[:, 0:2, :], row_cols[:, k, :, :, :], start=False, stop=False)
                for u in range(2):
                    for j in range(TPG):
                        last = pe.matmul(decay_ps[k][:, u, j, :], pick_row[:, NH * j + 2 * u + k, :, :],
                                         parts[:, 2, :], start=False, stop=(u == 1 and j == TPG - 1))
                return last

            pe.wait_ge(ident_ready, 1)

            def step(i):
                if works(i, 2):
                    g = i - 2
                    pe.wait_ge(normed_ready[A_], TPG * g + TPG)
                    if started(g):
                        pe.wait_ge(weighted, 2 * g)
                    for j in range(TPG):
                        last = pe.transpose(bank_q[:, P * j:P * j + P], normed[A_][:, j, :], ident[:, :])
                    last.then_inc(q_in_psum, 1)
                if works(i, 6):
                    g = i - 6
                    pe.wait_ge(att_t_ready, g + 1)
                    pe.wait_ge(ctx_c_loaded, 16 * (g + 1))
                    pe_takes_wait()
                    for j in range(TPG):
                        for half in HALVES:
                            last = pe.matmul(bank[5][half, P * j:P * j + P], att_t[half, j, :], ctx_c[half, j, :], start=True, stop=True)
                    last.then_inc(win_in_psum, 1)
                if works(i, 3):
                    g = i - 3
                    for j in range(TPG // 2, TPG):
                        for h in range(NH):
                            for half in HALVES:
                                last = pe.matmul(heads_ps[half, 1, NH * (j - TPG // 2) + h, :], weights[half, h % 2, h // 2, j, :],
                                                 v_aug[half, j, h, :], start=True, stop=True)
                    last.then_inc(heads_in_psum, 1)
                if works(i, 7):
                    g = i - 7
                    pe.wait_ge(x_k_ready, g + 1)
                    pe.matmul(bank[7], w_t[:, WK, :], x_k[:, :], start=True, stop=True).then_inc(k_in_psum, 1)
                if works(i, 5):
                    g = i - 5
                    pe.wait_ge(normed_ready[C_], TPG * g + TPG)
                    if started(g):
                        pe.wait_ge(stage_c_done, g)
                    for j in range(TPG):
                        last = pe.transpose(bank[5][:, P * j:P * j + P], normed[C_][:, j, :], ident[:, :])
                    last.then_inc(c_in_psum, 1)
                if works(i, 2):
                    g = i - 2
                    if first(g):
                        pe.wait_ge(gate_weights_ready, 1)
                    pe.wait_ge(q_t_ready, g + 1)
                    pe.wait_ge(ctx_t_ready, g + 1)
                    for j in range(TPG // 2):
                        pe.matmul(gates_ps[:, j, :], q_t[:, P * j:P * j + P], gate_w_q[:, :], start=True, stop=False)
                        last = pe.matmul(gates_ps[:, j, :], ctx_t[:, P * j:P * j + P], gate_w_c[:, :], start=False, stop=True)
                    last.then_inc(gates_in_psum, 1)
                    pe.wait_ge(q_t_ready, g + 1)
                    pe.wait_ge(ctx_t_ready, g + 1)
                    for j in range(TPG // 2, TPG):
                        pe.matmul(gates_ps[:, j, :], q_t[:, P * j:P * j + P], gate_w_q[:, :], start=True, stop=False)
                        last = pe.matmul(gates_ps[:, j, :], ctx_t[:, P * j:P * j + P], gate_w_c[:, :], start=False, stop=True)
                    last.then_inc(gates_in_psum, 1)
                if works(i, 5):
                    g = i - 5
                    pe.wait_ge(c_t_ready, g + 1)
                    if started(g):
                        pe.wait_ge(att_t_ready, g)
                    pe.matmul(bank[6][0:HID, :], w_t[:, WP, 0:HID], c_t[:, :], start=True, stop=True).then_inc(hid_in_psum, 1)
                if works(i, 2):
                    g = i - 2
                    if first(g):
                        pe.wait_ge(w_copied, 4)
                    pe.wait_ge(q_t_ready, g + 1)
                    pe.wait_ge(ctx_t_ready, g + 1)
                    pe.matmul(bank_q[:, :], w_t[:, WA, :], ctx_t[:, :], start=True, stop=True).then_inc(kw_in_psum, 1)
                if works(i, 5):
                    g = i - 5
                    pe.wait_ge(hid_ready, g + 1)
                    for j in range(TPG):
                        last = pe.matmul(z_ps[:, j:j + 1], hid[:, P * j:P * j + P], vp_col[:, :], start=True, stop=True)
                    last.then_inc(z_in_psum, 1)
                if works(i, 7):
                    g = i - 7
                    pe.wait_ge(x4_ready, 3 * g + 3)
                    pe.wait_ge(k_relu_ready, g + 1)
                    for j in range(TPG):
                        tokens = slice(P * j, P * j + P)
                        pe.matmul(bank[7][:, tokens], x_now[:, tokens], w_mix[:, 0, :], start=True, stop=False)
                        last = pe.matmul(bank[7][:, tokens], x_prev[:, 2 * j:2 * j + 2, :], w_mix[:, 1, :], start=False, stop=True)
                    last.then_inc(r_in_psum, 1)
                if works(i, 2):
                    g = i - 2
                    if first(g):
                        pe.wait_ge(consts_ready, 1)
                    pe.wait_ge(gates_exp_ready, g + 1)
                    pe.wait_ge(v_mean_ready, g + 1)
                    pe.matmul(rows_ps[:, 0, :], forget_exp, cum[:, :], start=True, stop=True)
                    pe.matmul(rows_ps[:, 1, :], input_exp, pick[:, :], start=True, stop=False)
                    pe.matmul(rows_ps[:, 1, :], forget_exp, neg_cum[:, :], start=False, stop=True).then_inc(rows_in_psum, 1)
                if works(i, 5):
                    g = i - 5
                    pe.wait_ge(kw_c_ready, g + 1)
                    pe.wait_ge(tanh_z_ready, g + 1)
                    for j in range(TPG):
                        for half in HALVES:
                            tokens = slice(P * j + half.start, P * j + half.stop)
                            last = pe.matmul(win_ps[half, j, :], c_t[:, tokens], kw_c[:, tokens], start=True, stop=True)
                    last.then_inc(win_scores_in_psum, 1)
                if works(i, 7):
                    g = i - 7
                    pe.wait_ge(k_act_ready, g + 1)
                    pe.wait_ge(r_tanh_ready, g + 1)
                    for j in range(TPG):
                        last = pe.matmul(bank[7][:, P * j:P * j + P], k_act[:, P * j:P * j + P], w_t[:, WV, :], start=True, stop=True)
                    last.then_inc(v_in_psum, 1)
                if works(i, 2):
                    g = i - 2
                    pe.wait_ge(kw_ready, g + 1)
                    pe.wait_ge(sum_row_ready, g + 1)
                    for h in (0, 1):
                        head = slice(DH * h, DH * h + DH)
                        for j in range(TPG):
                            for half in HALVES:
                                tokens = slice(P * j + half.start, P * j + half.stop)
                                last = pe.matmul(score_ps[h % 2][half, h // 2, j, :], ctx_t[head, tokens], q_t[head, tokens],
                                                 start=True, stop=True)
                        last.then_inc(head_scores_done, 1)
                    if first(g):
                        pe.wait_ge(weights_ready, 1)
                    if first(g):
                        pe.wait_ge(consts_ready, 3)
                        pe.wait_ge(consts_spread, 2)
                    pe.wait_ge(parts_ready, g + 1)
                    if started(g):
                        pe.wait_ge(h_n_ready, g)
                    decay_product(0).then_inc(decay_log_in_psum, 1)
                    if first(g):
                        pe.wait_ge(consts_ready, 3)
                        pe.wait_ge(consts_spread, 2)
                        pe.wait_ge(weights_ready, 1)
                    pe.wait_ge(parts_ready, g + 1)
                    if started(g):
                        pe.wait_ge(h_n_ready, g)
                    decay_product(1).then_inc(decay_log_in_psum, 1)
                if works(i, 4):
                    g = i - 4
                    pe.wait_ge(x_q_ready, g + 1)
                    if started(g):
                        pe.wait_ge(stage_b_done, g)
                    for j in range(TPG):
                        last = pe.transpose(xq_ps[:, P * j:P * j + P], x_q[:, j, :], ident_bf[:, :])
                    last.then_inc(x_q_in_psum, 1)
                if works(i, 2):
                    g = i - 2
                    pe.wait_ge(kw_ready, g + 1)
                    pe.wait_ge(sum_row_ready, g + 1)
                    for h in (2, 3):
                        head = slice(DH * h, DH * h + DH)
                        pe.wait_ge(head_scores_done, NH * g + h - 1)
                        for j in range(TPG):
                            for half in HALVES:
                                tokens = slice(P * j + half.start, P * j + half.stop)
                                last = pe.matmul(score_ps[h % 2][half, h // 2, j, :], ctx_t[head, tokens], q_t[head, tokens],
                                                 start=True, stop=True)
                        last.then_inc(head_scores_done, 1)
                if works(i, 4):
                    g = i - 4
                    pe.wait_ge(x_q_t_ready, g + 1)
                    pe.matmul(ffn_ps[:, :], ones_bf[:, :], bias_parts[:, :, :], start=True, stop=False)
                    for j in range(TPG):
                        for n in range(3):
                            last = pe.matmul(ffn_ps[:, P * j:P * j + P], x_q_t[:, P * j:P * j + P], w_parts[:, n, :], start=False,
                                             stop=(n == 2 and j == TPG - 1))
                    last.then_inc(ffn_in_psum, 1)
                if works(i, 6):
                    g = i - 6
                    pe.wait_ge(normed_ready[D_], TPG * g + TPG)
                    if started(g):
                        pe.wait_ge(y_ready, g)
                    for j in range(TPG):
                        last = pe.transpose(bank[7][:, P * j:P * j + P], normed[D_][:, j, :], ident[:, :])
                    last.then_inc(x4_in_psum, 1)
                if works(i, 5):
                    g = i - 5
                    pe.wait_ge(att_ready, g + 1)
                    pe_takes_wait()
                    for j in range(TPG):
                        for half in HALVES:
                            last = pe.matmul(att_ps[half, j, :], att[half, j, :], ident[half, half], start=True, stop=True)
                    last.then_inc(att_in_psum, 1)
                if works(i, 2):
                    g = i - 2
                    pe.wait_ge(weighted, 2 * g + 2)
                    pe.wait_ge(v_aug_ready, g + 1)
                    pe.wait_ge(exp_row_ready, g + 1)
                    for b, half in enumerate(HALVES):
                        pe.matmul(exp_col_ps[half, :], exp_row[0:32, :], back[:, b, :], start=True, stop=True)
                    for j in range(TPG // 2):
                        for h in range(NH):
                            for half in HALVES:
                                last = pe.matmul(heads_ps[half, 0, NH * j + h, :], weights[half, h % 2, h // 2, j, :],
                                                 v_aug[half, j, h, :], start=True, stop=True)
                    last.then_inc(heads_in_psum, 1)
                if works(i, 1):
                    g = i - 1
                    pe.wait_ge(ctx_a_loaded, 16 * (g + 1))
                    if started(g):
                        pe.wait_ge(weighted, 2 * g)
                    for j in range(TPG):
                        last = pe.transpose(bank_ctx[:, P * j:P * j + P], ctx_a[:, j, :], ident[:, :])
                    last.then_inc(ctx_in_psum, 1)
                    if first(g):
                        transpose_weights()

            steps(pe, step)



_INS = ['x', 'ctx_1024', 'L0_xattn_igate_kernel', 'L0_xattn_igate_bias', 'L0_xattn_fgate_kernel',
        'L0_xattn_fgate_bias', 'L0_xattn_outnorm_scale', 'L0_ffn_weight_fp8', 'L0_ffn_bias', 'L0_ffn_input_scale',
        'L0_ffn_weight_scale', 'L1_xattn_W_a', 'L1_xattn_W_p', 'L1_xattn_V_p', 'L1_ffn_W_r', 'L1_ffn_W_k',
        'L1_ffn_W_v', 'L1_ffn_mu_r', 'L1_ffn_mu_k']


def kernel(**inputs):
    import numpy as _np
    import concourse.bacc as _bacc
    from concourse import mybir as _mybir
    from concourse.bass_utils import run_bass_kernel_spmd as _run

    nc = _bacc.Bacc("TRN2", target_bir_lowering=False, num_devices=1)
    arrays, args = {}, []
    for name in _INS:
        a = _np.ascontiguousarray(inputs[name])
        arrays[f"in_{name}_dram"] = a
        args.append(nc.dram_tensor(f"in_{name}_dram", a.shape, _mybir.dt.from_np(a.dtype), kind="ExternalInput").ap())
    out = nc.dram_tensor("out_0_dram", tuple(inputs["x"].shape), _mybir.dt.float32, kind="ExternalOutput").ap()
    xattn_ffn_two_layers(nc, *args, out)
    r = _run(nc, [arrays], core_ids=[0])
    return r.results[0]["out_0_dram"]
```
